# Optimizing a Trainium2 kernel written in Bass

```python
import numpy as np
import jax
import jax.numpy as jnp

def _softmax(x, axis=-1):
    return jax.nn.softmax(x, axis=axis)

def _gelu(x):
    return jax.nn.gelu(x, approximate=True)

def _silu(x):
    return jax.nn.silu(x)

def _sigmoid(x):
    return jax.nn.sigmoid(x)

def _layernorm(x, axis=-1, eps=1e-05):
    m = jnp.mean(x, axis=axis, keepdims=True)
    v = jnp.var(x, axis=axis, keepdims=True)
    return (x - m) / jnp.sqrt(v + eps)

def _scatter_add(tgt, idx, src, axis=0):
    return tgt.at[idx].add(src)

def _segment_sum(src, seg, n):
    return jax.ops.segment_sum(src, seg, n)
kernel_name = 'mk_adaln_d1_jaxref_r4_66d669'

def setup_inputs(seed: int=0):
    np.random.seed(seed)
    _w = jnp.asarray

    def _L0_attn_setup():
        import jax, jax.numpy as jnp
        import numpy as np
        H = 16
        E = 256
        D = E // H
        M = 256
        EPS = 1e-12
        key = jax.random.key(seed)
        ks = jax.random.split(key, 12)
        s = 0.02
        B, S = (8, 256)
        return {'hidden_states': jax.random.normal(ks[0], (B, S, E), jnp.float32), 'Wq': jax.random.normal(ks[1], (E, E), jnp.float32) * s, 'bq': jnp.zeros((E,), jnp.float32), 'Wk': jax.random.normal(ks[2], (E, E), jnp.float32) * s, 'bk': jnp.zeros((E,), jnp.float32), 'Wv': jax.random.normal(ks[3], (E, E), jnp.float32) * s, 'bv': jnp.zeros((E,), jnp.float32), 'dist_emb': jax.random.normal(ks[4], (2 * M - 1, D), jnp.float32) * s, 'Wo': jax.random.normal(ks[5], (E, E), jnp.float32) * s, 'bo': jnp.zeros((E,), jnp.float32), 'ln_gamma': jnp.ones((E,), jnp.float32), 'ln_beta': jnp.zeros((E,), jnp.float32)}
    _L0_attn_in = _L0_attn_setup()

    def _L0_ffn_setup():
        import jax, jax.numpy as jnp
        import numpy as np
        B, T, D_IN, D_OUT = (4, 512, 256, 256)
        N_EXPERTS, N_ACTIVE = (8, 2)
        key = jax.random.key(seed)
        k1, k2, k3, k4, k5 = jax.random.split(key, 5)
        s_in = 1.0 / np.sqrt(D_IN)
        x = jax.random.normal(k1, (B, T, D_IN), dtype=jnp.float32)
        w_router = jax.random.uniform(k2, (N_EXPERTS, D_IN), jnp.float32, -s_in, s_in)
        b_router = jax.random.uniform(k3, (N_EXPERTS,), jnp.float32, -s_in, s_in)
        w_experts = jax.random.uniform(k4, (N_EXPERTS, D_OUT, D_IN), jnp.float32, -s_in, s_in)
        b_experts = jax.random.uniform(k5, (N_EXPERTS, D_OUT), jnp.float32, -s_in, s_in)
        return {'x': x, 'w_router': w_router, 'b_router': b_router, 'w_experts': w_experts, 'b_experts': b_experts}
    _L0_ffn_in = _L0_ffn_setup()
    _L0_c = _w((lambda *s: np.random.randn(*s).astype(np.float32) * 0.05)(16, 256))
    _L0_wmod = _w((lambda *s: np.random.randn(*s).astype(np.float32) * 0.05)(256, 6 * 256) * 256 ** (-0.5))
    _d = {'L0_attn_hidden_states': _L0_attn_in['hidden_states'], 'L0_attn_Wq': _L0_attn_in['Wq'], 'L0_attn_bq': _L0_attn_in['bq'], 'L0_attn_Wk': _L0_attn_in['Wk'], 'L0_attn_bk': _L0_attn_in['bk'], 'L0_attn_Wv': _L0_attn_in['Wv'], 'L0_attn_bv': _L0_attn_in['bv'], 'L0_attn_dist_emb': _L0_attn_in['dist_emb'], 'L0_attn_Wo': _L0_attn_in['Wo'], 'L0_attn_bo': _L0_attn_in['bo'], 'L0_attn_ln_gamma': _L0_attn_in['ln_gamma'], 'L0_attn_ln_beta': _L0_attn_in['ln_beta'], 'L0_ffn_w_router': _L0_ffn_in['w_router'], 'L0_ffn_b_router': _L0_ffn_in['b_router'], 'L0_ffn_w_experts': _L0_ffn_in['w_experts'], 'L0_ffn_b_experts': _L0_ffn_in['b_experts'], 'L0_c': _L0_c, 'L0_wmod': _L0_wmod}
    _x0 = _d['L0_attn_hidden_states']
    _d['L0_attn_hidden_states'] = jax.random.normal(jax.random.fold_in(jax.random.key(seed), 1), (16, 512, 256), dtype=_x0.dtype)
    del _x0
    return _d

def reference(L0_attn_hidden_states, L0_attn_Wq, L0_attn_bq, L0_attn_Wk, L0_attn_bk, L0_attn_Wv, L0_attn_bv, L0_attn_dist_emb, L0_attn_Wo, L0_attn_bo, L0_attn_ln_gamma, L0_attn_ln_beta, L0_ffn_w_router, L0_ffn_b_router, L0_ffn_w_experts, L0_ffn_b_experts, L0_c, L0_wmod):

    def _L0_attn_ref(hidden_states, Wq, bq, Wk, bk, Wv, bv, dist_emb, Wo, bo, ln_gamma, ln_beta):
        import jax, jax.numpy as jnp
        import numpy as np
        H = 16
        E = 256
        D = E // H
        M = 256
        EPS = 1e-12
        B, S, _ = hidden_states.shape

        def heads(x):
            return x.reshape(B, S, H, D).transpose(0, 2, 1, 3)
        q = heads(hidden_states @ Wq + bq)
        k = heads(hidden_states @ Wk + bk)
        v = heads(hidden_states @ Wv + bv)
        scores = jnp.einsum('bhqd,bhkd->bhqk', q, k)
        pos_l = jnp.arange(S)[:, None]
        pos_r = jnp.arange(S)[None, :]
        dist_idx = pos_l - pos_r + M - 1
        pos_emb = dist_emb[dist_idx]
        rel_q = jnp.einsum('bhld,lrd->bhlr', q, pos_emb)
        rel_k = jnp.einsum('bhrd,lrd->bhlr', k, pos_emb)
        scores = (scores + rel_q + rel_k) / jnp.sqrt(jnp.asarray(D, scores.dtype))
        probs = jax.nn.softmax(scores, axis=-1)
        ctx = jnp.einsum('bhqk,bhkd->bhqd', probs, v)
        ctx = ctx.transpose(0, 2, 1, 3).reshape(B, S, E)
        h = ctx @ Wo + bo + hidden_states
        mu = jnp.mean(h, axis=-1, keepdims=True)
        var = jnp.mean(jnp.square(h - mu), axis=-1, keepdims=True)
        out = (h - mu) * jax.lax.rsqrt(var + EPS) * ln_gamma + ln_beta
        return out

    def _L0_ffn_ref(x, w_router, b_router, w_experts, b_experts):
        import jax, jax.numpy as jnp
        import numpy as np
        B, T, D_IN, D_OUT = (4, 512, 256, 256)
        N_EXPERTS, N_ACTIVE = (8, 2)
        gamma = jax.nn.softmax(jnp.einsum('btd,ed->bte', x, w_router) + b_router, axis=-1)
        _, expert_ids = jax.lax.top_k(gamma, N_ACTIVE)
        mask = (expert_ids[..., None] == jnp.arange(N_EXPERTS)).any(axis=-2)
        y_all = jnp.einsum('btd,eod->bteo', x, w_experts) + b_experts
        y = jnp.einsum('bte,bteo->bto', mask.astype(x.dtype), y_all)
        return y
    x = L0_attn_hidden_states
    mod = (_silu(L0_c) @ L0_wmod).reshape(L0_c.shape[0], 6, 1, -1)
    sa, ca, ga, sb, cb, gb = (mod[:, 0], mod[:, 1], mod[:, 2], mod[:, 3], mod[:, 4], mod[:, 5])
    ga = (2 * (ga >= 0) - 1) * jnp.maximum(jnp.abs(ga), 0.25)
    gb = (2 * (gb >= 0) - 1) * jnp.maximum(jnp.abs(gb), 0.25)
    h = _layernorm(x, axis=-1) * (1 + ca) + sa
    x = x + ga * _L0_attn_ref(h, L0_attn_Wq, L0_attn_bq, L0_attn_Wk, L0_attn_bk, L0_attn_Wv, L0_attn_bv, L0_attn_dist_emb, L0_attn_Wo, L0_attn_bo, L0_attn_ln_gamma, L0_attn_ln_beta)
    h = _layernorm(x, axis=-1) * (1 + cb) + sb
    x = x + gb * _L0_ffn_ref(h, L0_ffn_w_router, L0_ffn_b_router, L0_ffn_w_experts, L0_ffn_b_experts)
    return x

_drawn_inputs = setup_inputs


def setup_inputs(seed=0):
    import zlib

    import numpy as np

    out = dict(_drawn_inputs(seed))
    spreads = {'L0_attn_bq': (0.0, 0.8),
     'L0_attn_bk': (0.0, 2.0),
     'L0_attn_bv': (0.0, 0.38),
     'L0_attn_bo': (0.0, 0.308),
     'L0_attn_ln_gamma': (1.0, 0.2),
     'L0_attn_ln_beta': (0.0, 0.1)}
    factors = {'L0_attn_Wq': 8.0,
     'L0_attn_Wk': 8.0,
     'L0_attn_Wv': 7.136,
     'L0_attn_dist_emb': 8.0,
     'L0_attn_Wo': 3.45,
     'L0_ffn_b_experts': 4.674}
    for name, (base, spread) in spreads.items():
        noise = np.random.default_rng([zlib.crc32(name.encode()), seed]).standard_normal(out[name].shape)
        drawn = base * np.exp(spread * noise) if base else spread * noise
        out[name] = jnp.asarray(drawn.astype(out[name].dtype))
    for name, factor in factors.items():
        out[name] = (out[name] * factor).astype(out[name].dtype)
    return out
```

```python
from contextlib import ExitStack

import concourse.bass as bass
from concourse import mybir

F32 = mybir.dt.float32
BF16 = mybir.dt.bfloat16
U32 = mybir.dt.uint32
ALU = mybir.AluOpType
ACT = mybir.ActivationFunctionType

P = 128
NB, S, E = 16, 512, 256
H = 16
D = E // H
M = 256
KC = E // P
TT = S // P
NE = 8
EPS_LN = 1e-5
EPS_ATTN = 1e-12

A_PARTS = (0, 1, 2, 0, 1, 0)
B_PARTS = (0, 0, 0, 1, 1, 2)
ROWS = len(A_PARTS) * D
SD = 3 * D

GB = P // H
NG = NB // GB
LW, RW = 64, 128
LC, RC = S // LW, S // RW
TAB = 2 * S
WIN = LW + RW
RPITCH = S * S + 1024

SA, CA1, GAG, GAB, SB, CB1, GB_ = range(7)
NMOD = 7


def later(engine, semaphore, value):
    if isinstance(value, int) and value <= 0:
        return
    engine.wait_ge(semaphore, value)


def rows_of(parts):
    runs, at = [], 0
    while at < len(parts):
        n = 1
        while at + n < len(parts) and parts[at + n] == parts[at] + n:
            n += 1
        runs.append((at * D, parts[at] * D, n * D))
        at += n
    return runs


A_RUNS, B_RUNS = rows_of(A_PARTS), rows_of(B_PARTS)


def modulation(nc, ins, mod_d, tab_d):
    ctx = ExitStack()
    with ctx:
        def sb(name, shape, dt=F32):
            return ctx.enter_context(nc.sbuf_tensor(name, shape, dt))

        def sem(name):
            return ctx.enter_context(nc.semaphore(name))

        cT = sb("m_cT", [P, KC, NB])
        en = sb("m_en", [P, KC, NB])
        den = sb("m_den", [P, KC, NB])
        rec = sb("m_rec", [P, KC, NB])
        act = sb("m_silu", [P, KC, NB])
        wmod = sb("m_wmod", [P, KC, 6 * E])
        gamma = sb("m_gamma", [NB, E])
        beta = sb("m_beta", [NB, E])
        up = sb("m_up", [NB, 2, E])
        dn = sb("m_dn", [NB, 2, E])
        pos = sb("m_pos", [NB, 2, E])
        neg = sb("m_neg", [NB, 2, E])
        gate = sb("m_gate", [NB, 2, E])
        mod = sb("m_mod", [NB, NMOD, E])
        eT = sb("m_eT", [D, 2 * M])
        t32 = sb("m_t32", [D, TAB])
        res = sb("m_res", [D, TAB])
        res2 = sb("m_res2", [D, TAB])
        parts = sb("m_parts", [D, 3, TAB], BF16)
        pm = ctx.enter_context(nc.psum_tensor("m_psum", [NB, 3, 512], F32))

        loaded = sem("m_loaded")
        e_loaded = sem("m_e_loaded")
        exp_done = sem("m_exp_done")
        silu_done = sem("m_silu_done")
        mod_product = sem("m_mod_product")
        step = sem("m_step")
        t_step = sem("m_t_step")
        mod_done = sem("m_mod_done")
        table_done = sem("m_table_done")
        stored = sem("m_stored")

        with nc.Block() as block:
            @block.sync
            def _(sp):
                sp.dma_start(cT[:], ins["cT"].rearrange("(k p) b -> p k b", p=P)).then_inc(loaded, 16)
                sp.dma_start(eT[:, 0:2 * M - 1], ins["eT"]).then_inc(e_loaded, 16)
                sp.dma_start(wmod[:], ins["wmod"].rearrange("(k p) n -> p k n", p=P)).then_inc(loaded, 16)
                sp.dma_start(gamma[:], ins["gamma"].partition_broadcast(NB)).then_inc(loaded, 16)
                sp.dma_start(beta[:], ins["beta"].partition_broadcast(NB)).then_inc(loaded, 16)
                sp.wait_ge(table_done, 1)
                for row, part in enumerate(B_PARTS):
                    sp.dma_start(tab_d[row * D:(row + 1) * D, :], parts[:, part, :]).then_inc(stored, 16)
                sp.wait_ge(mod_done, 1)
                sp.dma_start(mod_d[:, :, :], mod[:]).then_inc(stored, 16)
                sp.wait_ge(stored, 16 * (len(B_PARTS) + 1))

            @block.scalar
            def _(act_e):
                act_e.wait_ge(loaded, 64)
                nc.scalar.activation(en[:], cT[:], ACT.Exp, scale=-1.0).then_inc(exp_done, 1)

            @block.tensor
            def _(pe):
                pe.wait_ge(silu_done, 1)
                for n in range(3):
                    for k in range(KC):
                        last = nc.tensor.matmul(pm[:, n, :], act[:, k, :], wmod[:, k, n * 512:(n + 1) * 512],
                                                start=(k == 0), stop=(k == KC - 1))
                last.then_inc(mod_product, 1)

            @block.vector
            def _(dve):
                done = [0, 0]

                def then(instruction):
                    done[0] += 1
                    instruction.then_inc(step, 1)
                    dve.wait_ge(step, done[0])

                def then_t(instruction):
                    done[1] += 1
                    instruction.then_inc(t_step, 1)
                    dve.wait_ge(t_step, done[1])

                dve.wait_ge(exp_done, 1)
                then(nc.vector.tensor_scalar_add(den[:], en[:], 1.0))
                then(nc.vector.reciprocal(rec[:], den[:]))
                nc.vector.tensor_tensor(act[:], cT[:], rec[:], ALU.mult).then_inc(silu_done, 1)
                dve.wait_ge(e_loaded, 16)
                nc.vector.tensor_copy(t32[:, 0:M], eT[:, M - 1:2 * M - 1])
                nc.vector.tensor_copy(t32[:, M:3 * M - 1], eT[:, 0:2 * M - 1])
                then_t(nc.vector.tensor_copy(t32[:, 3 * M - 1:TAB], eT[:, 2 * M - 2:2 * M - 1].to_broadcast([D, TAB - 3 * M + 1])))
                then_t(nc.vector.tensor_copy(parts[:, 0, :], t32[:]))
                then_t(nc.vector.tensor_tensor(res[:], t32[:], parts[:, 0, :], ALU.subtract))
                then_t(nc.vector.tensor_copy(parts[:, 1, :], res[:]))
                nc.vector.tensor_tensor(parts[:, 2, :], res[:], parts[:, 1, :], ALU.subtract).then_inc(table_done, 1)
                dve.wait_ge(mod_product, 1)
                m6 = pm[:, :, :].rearrange("b n (a f) -> b (n a) f", a=2)
                nc.vector.tensor_copy(mod[:, SA, :], m6[:, 0, :])
                nc.vector.tensor_copy(mod[:, SB, :], m6[:, 3, :])
                nc.vector.tensor_scalar_add(mod[:, CA1, :], m6[:, 1, :], 1.0)
                nc.vector.tensor_scalar_add(mod[:, CB1, :], m6[:, 4, :], 1.0)
                for i, row in enumerate((2, 5)):
                    nc.vector.tensor_scalar(up[:, i, :], m6[:, row, :], 0.25, None, ALU.max)
                    nc.vector.tensor_scalar(dn[:, i, :], m6[:, row, :], -0.25, None, ALU.min)
                    nc.vector.tensor_scalar(pos[:, i, :], m6[:, row, :], 0.0, None, ALU.is_ge)
                    then(nc.vector.tensor_scalar(neg[:, i, :], m6[:, row, :], 0.0, None, ALU.is_lt))
                then(nc.vector.tensor_tensor(up[:], up[:], pos[:], ALU.mult))
                then(nc.vector.tensor_tensor(dn[:], dn[:], neg[:], ALU.mult))
                then(nc.vector.tensor_tensor(gate[:], up[:], dn[:], ALU.add))
                nc.vector.tensor_copy(mod[:, GB_, :], gate[:, 1, :])
                nc.vector.tensor_tensor(mod[:, GAG, :], gate[:, 0, :], gamma[:], ALU.mult)
                nc.vector.tensor_tensor(mod[:, GAB, :], gate[:, 0, :], beta[:], ALU.mult).then_inc(mod_done, 1)


def inverse_root(nc, then, y, v, root_of, s, t):
    root_of()
    then(nc.vector.reciprocal(y, s))
    then(nc.vector.tensor_tensor(t, y, y, ALU.mult))
    then(nc.vector.tensor_tensor(t, t, v, ALU.mult))
    then(nc.vector.tensor_scalar(t, t, -0.5, 1.5, ALU.mult, ALU.add))
    then(nc.vector.tensor_tensor(y, y, t, ALU.mult))


def projections(nc, ins, mod_d, h_d, qs_d, ks_d, qf_d, v_d, nb=NB):
    ctx = ExitStack()
    with ctx:
        def sb(name, shape, dt=F32):
            return ctx.enter_context(nc.sbuf_tensor(name, shape, dt))

        def ps(name, shape):
            return ctx.enter_context(nc.psum_tensor(name, shape, F32))

        def sem(name):
            return ctx.enter_context(nc.semaphore(name))

        wqk = sb("a_wqk", [P, 2, KC, E])
        wv = sb("a_wv", [P, KC, E])
        bqk = sb("a_bqk", [P, 2, KC])
        bv = sb("a_bv", [P, E])
        ident = sb("a_ident", [P, P])
        x = sb("a_x", [P, 2, TT, E])
        md = sb("a_mod", [P, 2, 2, E])
        st = sb("a_stats", [P, 2, TT, 6])
        mv = sb("a_mv", [P, 2, TT, 2])
        var = sb("a_var", [P, 2, TT])
        root = sb("a_root", [P, 2, TT])
        inv = sb("a_inv", [P, 2, TT])
        tmp = sb("a_tmp", [P, 2, TT])
        xn = sb("a_xn", [P, 2, TT, E])
        h = sb("a_h", [P, 2, TT, E])
        hT = sb("a_hT", [P, 2, KC, S])
        q32 = sb("a_q32", [P, 2, KC, S])
        rest = sb("a_rest", [P, 2, KC, S])
        part = sb("a_part", [P, 2, 2, 3, KC, S], BF16)
        vs = sb("a_v", [P, 2, H, TT, D])
        pT = ps("a_pT", [P, KC, S])
        pQ = ps("a_pQ", [P, 2, KC, S])
        pV = ps("a_pV", [P, TT, E])

        w_loaded = sem("a_w_loaded")
        ident_zero = sem("a_ident_zero")
        ident_done = sem("a_ident_done")
        x_loaded = [sem(f"a_x_loaded{u}") for u in range(2)]
        root_in = sem("a_root_in")
        root_out = sem("a_root_out")
        step = sem("a_step")
        xn_done = sem("a_xn_done")
        h_step = sem("a_h_step")
        h_done = sem("a_h_done")
        tr_done = sem("a_tr_done")
        hT_done = sem("a_hT_done")
        qk_done = sem("a_qk_done")
        v_done = sem("a_v_done")
        q32_done = sem("a_q32_done")
        part0_done = sem("a_part0_done")
        rest_done = sem("a_rest_done")
        part1_done = sem("a_part1_done")
        part2_done = sem("a_part2_done")
        vs_done = sem("a_vs_done")
        h_stored = [sem(f"a_h_stored{u}") for u in range(2)]
        q_stored = [sem(f"a_q_stored{u}") for u in range(2)]
        v_stored = [sem(f"a_v_stored{u}") for u in range(2)]

        x_v = ins["x"].rearrange("b (t p) e -> b p t e", p=P)
        h_v = h_d.rearrange("b (t p) e -> b p t e", p=P)

        with nc.Block() as block:
            @block.sync
            def _(sp):
                for i, name in enumerate(("wq", "wk")):
                    sp.dma_start(wqk[:, i], ins[name].rearrange("(k p) n -> p k n", p=P)).then_inc(w_loaded, 16)
                    sp.dma_start(bqk[:, i], ins["b" + name[1]]).then_inc(w_loaded, 16)
                sp.dma_start(wv[:], ins["wv"].rearrange("(k p) n -> p k n", p=P)).then_inc(w_loaded, 16)
                sp.dma_start(bv[:], ins["bv"].partition_broadcast(P)).then_inc(w_loaded, 16)

                def load(pair, u):
                    b = 2 * pair + u
                    later(sp, h_done, b - 1)
                    sp.dma_start(x[:, u], x_v[b]).then_inc(x_loaded[u], 16)
                    sp.dma_start(md[:, u], mod_d[b, SA:CA1 + 1, :].partition_broadcast(P)).then_inc(x_loaded[u], 16)

                def store(pair, u):
                    b = 2 * pair + u
                    g, b8 = b // GB, b % GB
                    sp.wait_ge(h_done, b + 1)
                    sp.dma_start(h_v[b], h[:, u]).then_inc(h_stored[u], 16)
                    sp.wait_ge(vs_done, b + 1)
                    sp.dma_start(v_d[b], vs[:, u].rearrange("p h t d -> p (h t d)")).then_inc(v_stored[u], 16)
                    for i, dsts in enumerate((((qs_d, LW), (qf_d, S)), ((ks_d, RW),))):
                        sp.wait_ge(part0_done, 2 * b + i + 1)
                        sp.wait_ge(part1_done, 2 * b + i + 1)
                        sp.wait_ge(part2_done, 2 * b + i + 1)
                        for (dst, w), s, c in ((dw, s, c) for dw in dsts for s in range(3) for c in range(KC)):
                                to = dst[g, :, b8, s * D + c * (D // KC):s * D + (c + 1) * (D // KC), :, :]
                                sp.dma_start(to.rearrange("n d h w -> (d h) n w"),
                                             part[:, u, i, s, c, :].rearrange("p (n w) -> p n w", w=w)
                                             ).then_inc(q_stored[u], 16)

                load(0, 0)
                load(0, 1)
                for u in range(2):
                    load(1, u)
                    store(0, u)
                with sp.Fori(1, nb // 2 - 1) as pair:
                    for u in range(2):
                        load(pair + 1, u)
                        store(pair, u)
                for u in range(2):
                    store(nb // 2 - 1, u)
                for u in range(2):
                    sp.wait_ge(h_stored[u], 16 * (nb // 2))
                    sp.wait_ge(v_stored[u], 16 * (nb // 2))
                    sp.wait_ge(q_stored[u], 16 * 18 * (nb // 2))

            @block.gpsimd
            def _(pool):
                nc.gpsimd.memset(ident[:], 0.0).then_inc(ident_zero, 1)
                pool.wait_ge(ident_zero, 1)
                nc.gpsimd.affine_select(out=ident[:], in_=ident[:], compare_op=ALU.not_equal, fill=1.0,
                                        base=0, pattern=[[-1, P]], channel_multiplier=1).then_inc(ident_done, 1)

                def modulate(pair, u):
                    b = 2 * pair + u
                    pool.wait_ge(xn_done, b + 1)
                    later(pool, tr_done, b - 1)
                    later(pool, h_stored[u], 16 * pair)
                    nc.gpsimd.tensor_tensor(h[:, u], xn[:, u], md[:, u, 1:2, :].to_broadcast([P, TT, E]),
                                            ALU.mult).then_inc(h_step, 1)
                    pool.wait_ge(h_step, b + 1)
                    nc.gpsimd.tensor_tensor(h[:, u], h[:, u], md[:, u, 0:1, :].to_broadcast([P, TT, E]),
                                            ALU.add).then_inc(h_done, 1)

                for u in range(2):
                    modulate(0, u)
                with pool.Fori(1, nb // 2) as pair:
                    for u in range(2):
                        modulate(pair, u)

            @block.tensor
            def _(pe):
                pe.wait_ge(ident_done, 1)
                pe.wait_ge(w_loaded, 96)

                def project(pair, u):
                    b = 2 * pair + u
                    pe.wait_ge(h_done, b + 1)
                    later(pe, hT_done, b)
                    for t in range(TT):
                        for c in range(KC):
                            last = nc.tensor.transpose(pT[:, c, t * P:(t + 1) * P], h[:, u, t, c * P:(c + 1) * P],
                                                       ident[:])
                    last.then_inc(tr_done, 1)
                    pe.wait_ge(hT_done, b + 1)
                    for i in range(2):
                        later(pe, q32_done, 2 * (b - 1) + i + 1)
                        for c in range(KC):
                            for k in range(KC):
                                last = nc.tensor.matmul(pQ[:, i, c, :], wqk[:, i, k, c * P:(c + 1) * P],
                                                        hT[:, u, k, :], start=(k == 0), stop=(k == KC - 1))
                        last.then_inc(qk_done, 1)
                    later(pe, vs_done, b)
                    for t in range(TT):
                        for k in range(KC):
                            last = nc.tensor.matmul(pV[:, t, :], hT[:, u, k, t * P:(t + 1) * P], wv[:, k, :],
                                                    start=(k == 0), stop=(k == KC - 1))
                    last.then_inc(v_done, 1)

                for u in range(2):
                    project(0, u)
                with pe.Fori(1, nb // 2) as pair:
                    for u in range(2):
                        project(pair, u)

            @block.scalar
            def _(act):
                act.wait_ge(w_loaded, 96)

                def take_root(pair, u):
                    b = 2 * pair + u
                    act.wait_ge(root_in, b + 1)
                    nc.scalar.activation(root[:, u], var[:, u], ACT.Sqrt).then_inc(root_out, 1)

                def split(pair, u):
                    b = 2 * pair + u
                    act.wait_ge(tr_done, b + 1)
                    later(act, v_done, b - 1)
                    nc.scalar.activation(hT[:, u], pT[:], ACT.Copy).then_inc(hT_done, 1)
                    for i in range(2):
                        act.wait_ge(qk_done, 2 * b + i + 1)
                        later(act, rest_done, 2 * (b - 1) + i + 1)
                        later(act, part0_done, 2 * (b - 1) + i + 1)
                        for c in range(KC):
                            last = nc.scalar.activation(q32[:, i, c, :], pQ[:, i, c, :], ACT.Identity,
                                                        bias=bqk[:, i, c:c + 1])
                        last.then_inc(q32_done, 1)
                        act.wait_ge(q32_done, 2 * b + i + 1)
                        later(act, q_stored[u], 16 * 18 * pair)
                        nc.scalar.activation(part[:, u, i, 0], q32[:, i], ACT.Copy).then_inc(part0_done, 1)
                    for i in range(2):
                        act.wait_ge(rest_done, 2 * b + i + 1)
                        nc.scalar.activation(part[:, u, i, 1], rest[:, i], ACT.Copy).then_inc(part1_done, 1)

                take_root(0, 0)
                take_root(0, 1)
                for u in range(2):
                    split(0, u)
                    take_root(1, u)
                with act.Fori(1, nb // 2 - 1) as pair:
                    for u in range(2):
                        split(pair, u)
                        take_root(pair + 1, u)
                for u in range(2):
                    split(nb // 2 - 1, u)

            @block.vector
            def _(dve):
                dve.wait_ge(w_loaded, 96)
                NSTEP = 7

                def normalise(pair, u):
                    b = 2 * pair + u
                    count = [0]

                    def then(instruction):
                        count[0] += 1
                        instruction.then_inc(step, 1)
                        dve.wait_ge(step, NSTEP * b + count[0])

                    def root_of():
                        dve.wait_ge(root_out, b + 1)

                    dve.wait_ge(x_loaded[u], 32 * (pair + 1))
                    for t in range(TT):
                        last = nc.vector.bn_stats(st[:, u, t, :], x[:, u, t, :])
                    then(last)
                    nc.vector.memset(tmp[:, u], 0.0)
                    for t in range(TT):
                        last = nc.vector.bn_aggr(mv[:, u, t, :], st[:, u, t, :])
                    then(last)
                    nc.vector.tensor_scalar_add(var[:, u], mv[:, u, :, 1], EPS_LN).then_inc(root_in, 1)
                    inverse_root(nc, then, inv[:, u], var[:, u], root_of, root[:, u], tmp[:, u])
                    later(dve, h_step, b - 1)
                    for t in range(TT):
                        last = nc.vector.tensor_scalar(xn[:, u, t, :], x[:, u, t, :], mv[:, u, t, 0:1],
                                                       inv[:, u, t:t + 1], ALU.subtract, ALU.mult)
                    last.then_inc(xn_done, 1)
                    assert count[0] == NSTEP

                def split(pair, u):
                    b = 2 * pair + u
                    for i in range(2):
                        dve.wait_ge(part0_done, 2 * b + i + 1)
                        later(dve, part2_done, 2 * (b - 1) + i + 1)
                        nc.vector.tensor_tensor(rest[:, i], q32[:, i], part[:, u, i, 0], ALU.subtract
                                                ).then_inc(rest_done, 1)
                    dve.wait_ge(v_done, b + 1)
                    later(dve, v_stored[u], 16 * pair)
                    for t in range(TT):
                        last = nc.vector.tensor_tensor(vs[:, u, :, t, :], pV[:, t, :].rearrange("p (h d) -> p h d", d=D),
                                                       bv[:].rearrange("p (h d) -> p h d", d=D), ALU.add)
                    last.then_inc(vs_done, 1)
                    for i in range(2):
                        dve.wait_ge(part1_done, 2 * b + i + 1)
                        nc.vector.tensor_tensor(part[:, u, i, 2], rest[:, i], part[:, u, i, 1], ALU.subtract
                                                ).then_inc(part2_done, 1)

                normalise(0, 0)
                normalise(0, 1)
                for u in range(2):
                    split(0, u)
                    normalise(1, u)
                with dve.Fori(1, nb // 2 - 1) as pair:
                    for u in range(2):
                        split(pair, u)
                        normalise(pair + 1, u)
                for u in range(2):
                    split(nb // 2 - 1, u)


def distances(nc, tab_d, qs_d, ks_d, r_d, ng=NG):
    ctx = ExitStack()
    with ctx:
        def sb(name, shape, dt=F32):
            return ctx.enter_context(nc.sbuf_tensor(name, shape, dt))

        def sem(name):
            return ctx.enter_context(nc.semaphore(name))

        UNIT = 1024
        QL = UNIT // RW
        KR = UNIT // LW
        NU = LW * RW // UNIT
        q = [sb(f"d_q{u}", [ROWS, P, LW], BF16) for u in range(2)]
        k = [sb(f"d_k{u}", [ROWS, P, RW], BF16) for u in range(2)]
        win = [sb(f"d_win{u}", [ROWS, WIN], BF16) for u in range(4)]
        r = [sb(f"d_r{u}", [P, LW, RW]) for u in range(2)]
        pq = [ctx.enter_context(nc.psum_tensor(f"d_pq{u}", [P, QL, RW], F32)) for u in range(2)]
        pk = [ctx.enter_context(nc.psum_tensor(f"d_pk{u}", [P, KR, LW], F32)) for u in range(2)]

        q_loaded = [sem(f"d_q_loaded{u}") for u in range(2)]
        k_loaded = [sem(f"d_k_loaded{u}") for u in range(2)]
        win_loaded = [sem(f"d_win_loaded{u}") for u in range(4)]
        q_units = sem("d_q_units")
        k_units = sem("d_k_units")
        q_even_out = sem("d_q_even_out")
        q_odd_out = sem("d_q_odd_out")
        k_added = sem("d_k_added")
        q_free = sem("d_q_free")
        r_stored = [sem(f"d_r_stored{u}") for u in range(2)]

        RH = RC // 2
        LCP = LC // 2
        NHALF = ng * RH

        with nc.Block() as block:
            @block.gpsimd
            def _(pool):
                def load_k(half, v):
                    later(pool, k_units, NU * (16 * half - 1 + v) * bool(half) if isinstance(half, int) else NU * (16 * half - 1 + v))
                    for row, stored, rows in A_RUNS:
                        src = ks_d[half // RH, (half % RH) * 2 + v, :, stored:stored + rows, :, :]
                        pool.dma_start(k[v][row:row + rows, :, :].rearrange("r (b h) w -> r b (h w)", b=GB),
                                       src.rearrange("b r h w -> r b (h w)")).then_inc(k_loaded[v], 16)

                def load_q(half, lcp, u):
                    later(pool, k_units, NU * (16 * half + 4 * lcp + 2 * u - 2))
                    for row, stored, rows in A_RUNS:
                        src = qs_d[half // RH, 2 * lcp + u, :, stored:stored + rows, :, :]
                        pool.dma_start(q[u][row:row + rows, :, :].rearrange("r (b h) w -> r b (h w)", b=GB),
                                       src.rearrange("b r h w -> r b (h w)")).then_inc(q_loaded[u], 16)
                    for v in range(2):
                        col = (2 * lcp + u) * LW - ((half % RH) * 2 + v) * RW + S - RW
                        pool.dma_start(win[2 * u + v][:], tab_d[:, bass.ds(col, WIN)]).then_inc(win_loaded[2 * u + v], 16)

                def body(half, first):
                    for v in range(2):
                        load_k(half, v)
                    if first:
                        for u in range(2):
                            load_q(half, 0, u)
                        with pool.Fori(1, LCP) as lcp:
                            for u in range(2):
                                load_q(half, lcp, u)
                    else:
                        with pool.Fori(0, LCP) as lcp:
                            for u in range(2):
                                load_q(half, lcp, u)

                body(0, True)
                with pool.Fori(1, NHALF) as half:
                    body(half, False)

            @block.tensor
            def _(pe):
                def chunk(at, u, v):
                    i = 4 * at + 2 * u + v
                    pe.wait_ge(q_loaded[u], 16 * len(A_RUNS) * (at + 1))
                    pe.wait_ge(win_loaded[2 * u + v], 16 * (at + 1))
                    for n in range(NU):
                        if n % 2 == 0:
                            later(pe, q_even_out, NU // 2 * i + n // 2)
                        else:
                            later(pe, q_odd_out, NU // 2 * i + n // 2)
                        for a in range(QL):
                            l = n * QL + a
                            rhs = bass.AP(win[2 * u + v], l + RW - 1, [[WIN, ROWS], [-1, RW]])
                            last = nc.tensor.matmul(pq[n % 2][:, a, :], q[u][:, :, l], rhs, start=True, stop=True)
                        last.then_inc(q_units, 1)
                    pe.wait_ge(k_loaded[v], 16 * len(A_RUNS) * (at // LCP + 1))
                    for n in range(NU):
                        later(pe, k_added, NU * i + n - 1)
                        for a in range(KR):
                            c = n * KR + a
                            last = nc.tensor.matmul(pk[n % 2][:, a, :], k[v][:, :, c],
                                                    win[2 * u + v][:, RW - 1 - c:RW - 1 - c + LW], start=True, stop=True)
                        last.then_inc(k_units, 1)

                def pair(at):
                    for u in range(2):
                        for v in range(2):
                            chunk(at, u, v)

                pair(0)
                with pe.Fori(1, NHALF * LCP) as at:
                    pair(at)

            @block.scalar
            def _(act):
                def chunk(i4, j):
                    i = 4 * i4 + j
                    later(act, r_stored[j % 2], 16 * (2 * i4 + j // 2))
                    for n in range(0, NU, 2):
                        act.wait_ge(q_units, NU * i + n + 1)
                        nc.scalar.activation(r[j % 2][:, n * QL:(n + 1) * QL, :], pq[0][:], ACT.Copy).then_inc(q_even_out, 1)

                for j in range(4):
                    chunk(0, j)
                with act.Fori(1, NHALF * LCP) as i4:
                    for j in range(4):
                        chunk(i4, j)

            @block.vector
            def _(dve):
                def chunk(i4, j):
                    i = 4 * i4 + j
                    later(dve, r_stored[j % 2], 16 * (2 * i4 + j // 2))
                    for n in range(1, NU, 2):
                        dve.wait_ge(q_units, NU * i + n + 1)
                        nc.vector.tensor_copy(r[j % 2][:, n * QL:(n + 1) * QL, :], pq[1][:]).then_inc(q_odd_out, 1)
                    dve.wait_ge(q_even_out, NU // 2 * (i + 1))
                    dve.wait_ge(q_odd_out, NU // 2 * (i + 1))
                    for n in range(NU):
                        dve.wait_ge(k_units, NU * i + n + 1)
                        part = r[j % 2][:, :, n * KR:(n + 1) * KR]
                        nc.vector.tensor_tensor(part, pk[n % 2][:].rearrange("p r l -> p l r"), part, ALU.add
                                                ).then_inc(k_added, 1)

                for j in range(4):
                    chunk(0, j)
                with dve.Fori(1, NHALF * LCP) as i4:
                    for j in range(4):
                        chunk(i4, j)

            @block.sync
            def _(sp):
                for g in range(ng):
                    with sp.Fori(0, RH * LCP) as at:
                        i4 = at + g * RH * LCP
                        for u in range(2):
                            for v in range(2):
                                sp.wait_ge(k_added, NU * (4 * i4 + 2 * u + v + 1))
                                to = r_d[g][:, bass.ts(2 * (at % LCP) + u, LW), bass.ts((at // LCP) * 2 + v, RW)]
                                sp.dma_start(to, r[v][:]).then_inc(r_stored[v], 16)
                for v in range(2):
                    sp.wait_ge(r_stored[v], 16 * 2 * NHALF * LCP)


def attention(nc, qf_d, ks_d, v_d, r_d, cT_d, nb=NB):
    ctx = ExitStack()
    with ctx:
        def sb(name, shape, dt=F32):
            return ctx.enter_context(nc.sbuf_tensor(name, shape, dt))

        def ps(name, shape):
            return ctx.enter_context(nc.psum_tensor(name, shape, F32))

        def sem(name):
            return ctx.enter_context(nc.semaphore(name))

        GH = 4
        CT = P // GH
        U = 2 * GH
        RR = 4
        AHEAD = 1
        SLOTS = 2 * H
        NH, NGR = nb * H, nb * H // GH
        BG = H // GH
        ident = sb("t_ident", [P, P])
        qa = sb("t_qa", [ROWS, 1, SLOTS, S], BF16)
        kb = sb("t_kb", [ROWS, RC, SLOTS, RW], BF16)
        vv = sb("t_v", [P, 2, GH, TT, D])
        r = sb("t_r", [P, RR, TT, S])
        neg = sb("t_neg", [P, TT, S])
        low = sb("t_low", [P, 2, TT])
        e = sb("t_e", [P, 2, TT, S])
        total = sb("t_total", [P, 2, TT, GH])
        inv = sb("t_inv", [P, 2, TT, GH])
        wide = sb("t_wide", [P, TT * GH, CT])
        ones = sb("t_ones", [P, TT * GH])
        wideT = sb("t_wideT", [P, S])
        eT = sb("t_eT", [P, 2, GH, TT, TT, P])
        out = sb("t_out", [P, 2, S])
        tiny = sb("t_tiny", [P, 8])
        p_s = [ps(f"t_ps{i}", [P, S]) for i in range(2)]
        p_t = [ps(f"t_pt{i}", [P, TT, P]) for i in range(TT)]
        p_c = ps("t_pc", [P, S])
        p_i = ps("t_pi", [P, S])

        ident_zero = sem("t_ident_zero")
        ident_done = sem("t_ident_done")
        batch_loaded = [sem(f"t_batch_loaded{i}") for i in range(2)]
        BATCH = 16 * (len(A_RUNS) + len(B_RUNS))
        v_loaded = [sem(f"t_v_loaded{i}") for i in range(2)]
        r_loaded = [sem(f"t_r_loaded{i}") for i in range(RR * TT)]
        scored = sem("t_scored")
        added = sem("t_added")
        exped = sem("t_exped")
        turned = sem("t_turned")
        even_out = sem("t_even_out")
        odd_out = sem("t_odd_out")
        pc_zero = sem("t_pc_zero")
        weighed = sem("t_weighed")
        inverted = sem("t_inverted")
        widened = sem("t_widened")
        wide_turned = sem("t_wide_turned")
        wide_out = sem("t_wide_out")
        ctx_done = sem("t_ctx_done")
        ctx_stored = [sem(f"t_ctx_stored{i}") for i in range(2)]

        with nc.Block() as block:
            @block.gpsimd
            def _(pool):
                nc.gpsimd.memset(ones[:], 1.0).then_inc(ident_zero, 1)
                nc.gpsimd.memset(ident[:], 0.0).then_inc(ident_zero, 1)
                pool.wait_ge(ident_zero, 2)
                nc.gpsimd.affine_select(out=ident[:], in_=ident[:], compare_op=ALU.not_equal, fill=1.0,
                                        base=0, pattern=[[-1, P]], channel_multiplier=1).then_inc(ident_done, 1)

                def load(pair, u):
                    b = 2 * pair + u
                    g, b8 = b // GB, b % GB
                    for tensor, src, runs in ((qa, qf_d, A_RUNS), (kb, ks_d, B_RUNS)):
                        for row, stored, rows in runs:
                            pool.dma_start(tensor[row:row + rows, :, u * H:(u + 1) * H, :].rearrange("r n h w -> r n (h w)"),
                                           src[g, :, b8, stored:stored + rows, :, :].rearrange("n r h w -> r n (h w)")
                                           ).then_inc(batch_loaded[u], 16)

                def widen(G, par):
                    pool.wait_ge(inverted, G + 1)
                    later(pool, wide_turned, G)
                    narrow = inv[:, par].rearrange("p l j -> p (l j)").unsqueeze(2).to_broadcast([P, TT * GH, CT])
                    nc.gpsimd.tensor_tensor(wide[:], narrow, ones[:].unsqueeze(2).to_broadcast([P, TT * GH, CT]),
                                            ALU.mult).then_inc(widened, 1)

                def store(b, k):
                    pool.wait_ge(ctx_done, BG * b + k + 1)
                    for j in range(GH):
                        row = (GH * k + j) * D
                        pool.dma_start(cT_d[b, row:row + D, :], out[j * CT:j * CT + D, k % 2, :]
                                       ).then_inc(ctx_stored[k % 2], 16)

                def batch(pair, u, more=True):
                    b = 2 * pair + u
                    for k in range(BG):
                        if more or k + 1 < BG:
                            widen(BG * b + k + 1, (k + 1) % 2)
                        if more and k == BG - 1 and (not isinstance(pair, int) or b + 2 < nb):
                            pool.wait_ge(scored, TT * H * (b + 1))
                            load(pair + 1, u)
                        store(b, k)

                for u in range(2):
                    load(0, u)
                widen(0, 0)
                with pool.Fori(0, nb // 2 - 1) as pair:
                    for u in range(2):
                        batch(pair, u)
                for u in range(2):
                    batch(nb // 2 - 1, u, more=(u == 0))
                for par in range(2):
                    pool.wait_ge(ctx_stored[par], 16 * GH * NGR // 2)

            @block.sync
            def _(sp):
                def load_r(g, n, j):
                    for L in range(TT):
                        later(sp, added, TT * (n - RR) + L + 1)
                        sp.dma_start(r[:, j % RR, L, :], r_d[g][n - g * P, L * P:(L + 1) * P, :]
                                     ).then_inc(r_loaded[j % RR * TT + L], 16)

                def load_v(G, b, k):
                    later(sp, weighed, TT * (G - 1))
                    sp.dma_start(vv[:, k % 2].rearrange("p h t d -> p (h t d)"),
                                 v_d[b, :, k * GH:(k + 1) * GH].rearrange("p h t d -> p (h t d)")
                                 ).then_inc(v_loaded[k % 2], 16)

                def heads(g, b, half):
                    for j in range(U):
                        load_r(g, H * b + U * half + j, j)
                        if j % GH == GH - 1:
                            k = (U * half + j) // GH
                            load_v(BG * b + k, b, k)

                for half in range(2):
                    heads(0, 0, half)
                for g in range((nb + GB - 1) // GB):
                    with sp.Fori(max(1, g * GB), min((g + 1) * GB, nb)) as b:
                        for half in range(2):
                            heads(g, b, half)

            @block.tensor
            def _(pe):
                pe.wait_ge(ident_done, 1)
                pe.wait_ge(pc_zero, 1)

                def score(n, L, slot):
                    later(pe, added, TT * n + L - 1)
                    nc.tensor.matmul(p_s[L % 2][:], qa[:, 0, slot, L * P:(L + 1) * P], kb[:, :, slot, :],
                                     start=True, stop=True).then_inc(scored, 1)

                def turn(n, j, L):
                    t = TT * n + L
                    pe.wait_ge(exped, t + 1)
                    later(pe, (even_out, odd_out)[L % 2], TT // 2 * (n - 1) + L // 2 + 1)
                    for c in range(TT):
                        last = nc.tensor.transpose(p_t[L][:, c, :], e[:, j % 2, L, c * P:(c + 1) * P], ident[:])
                    last.then_inc(turned, 1)

                def weigh(G, par, c, loads):
                    if c == 0:
                        pe.wait_ge(even_out, TT // 2 * GH * (G + 1))
                        pe.wait_ge(odd_out, TT // 2 * GH * (G + 1))
                        pe.wait_ge(v_loaded[par], 16 * loads)
                        later(pe, ctx_done, G)
                    for j in range(GH):
                        last = nc.tensor.matmul(p_c[j * CT:j * CT + D, :], vv[:, par, j, c, :],
                                                eT[:, par, j, c].rearrange("p l q -> p (l q)"),
                                                start=(c == 0), stop=(c == TT - 1))
                    last.then_inc(weighed, 1)

                def turn_wide(G, L):
                    if L == 0:
                        pe.wait_ge(widened, G + 1)
                        later(pe, wide_out, G)
                    last = nc.tensor.transpose(p_i[:, L * P:(L + 1) * P],
                                               wide[:, L * GH:(L + 1) * GH, :].rearrange("p j w -> p (j w)"), ident[:])
                    if L == TT - 1:
                        last.then_inc(wide_turned, 1)

                def head(step, j):
                    n = U * step + j
                    fixed = isinstance(n, int)
                    for L in range(TT):
                        m, M = n + (L + AHEAD) // TT, (L + AHEAD) % TT
                        if not fixed or m < NH:
                            score(m, M, m % SLOTS)
                        if not fixed or 1 <= n <= NH:
                            turn(n - 1, (j - 1) % U, L)
                        if L == 3 and (not fixed or 5 <= n < NH + 5):
                            ahead = (j - 5) // GH
                            weigh(2 * step + ahead, ahead % 2, (j - 5) % GH, step + ahead // 2 + 1)
                        if j % GH == 2 and (not fixed or 6 <= n < NH + 6):
                            turn_wide(2 * step + (j - 6) // GH, L)

                pe.wait_ge(batch_loaded[0], BATCH)
                for L in range(AHEAD):
                    score(0, L, 0)
                for step in range(H // U):
                    if step == H // U - 1:
                        pe.wait_ge(batch_loaded[1], BATCH)
                    for j in range(U):
                        head(step, j)
                with pe.Fori(H // U, NH // U - 1) as step:
                    pe.wait_ge(batch_loaded[0], BATCH * ((step + 1) // (SLOTS // U) + 1))
                    pe.wait_ge(batch_loaded[1], BATCH * ((step + 1 + H // U) // (SLOTS // U)))
                    for j in range(U):
                        head(step, j)
                for j in range(U):
                    head(NH // U - 1, j)
                for j in range(GH + 1):
                    head(NH // U, j)

            @block.vector
            def _(dve):
                nc.vector.memset(p_c[:], 0.0).then_inc(pc_zero, 1)

                def add(n, j, L, loads):
                    t = TT * n + L
                    dve.wait_ge(scored, t + 1)
                    dve.wait_ge(r_loaded[j % RR * TT + L], 16 * loads)
                    later(dve, exped, t - TT + 1)
                    nc.vector.memset(tiny[:, L:L + 1], 0.0)
                    nc.vector.tensor_tensor_reduce(out=neg[:, L, :], in0=p_s[L % 2][:], in1=r[:, j % RR, L, :], scale=-0.25,
                                                   scalar=3.0e38, op0=ALU.add, op1=ALU.min,
                                                   accum_out=low[:, j % 2, L:L + 1]).then_inc(added, 1)

                def empty(n, j, L, G):
                    dve.wait_ge(turned, TT * n + L + 1)
                    later(dve, weighed, TT * (G - 1))
                    nc.vector.tensor_copy(eT[:, j // GH, j % GH, :, L, :], p_t[L][:]).then_inc(odd_out, 1)

                def invert(G, par):
                    dve.wait_ge(exped, TT * GH * (G + 1))
                    later(dve, widened, G - 1)
                    nc.vector.reciprocal(inv[:, par], total[:, par]).then_inc(inverted, 1)

                def scale(G, par, stores):
                    dve.wait_ge(weighed, TT * (G + 1))
                    dve.wait_ge(wide_out, G + 1)
                    later(dve, ctx_stored[par], 16 * GH * stores)
                    nc.vector.tensor_tensor(out[:, par, :], p_c[:], wideT[:], ALU.mult).then_inc(ctx_done, 1)

                def head(step, j):
                    n = U * step + j
                    fixed = isinstance(n, int)
                    for L in range(TT):
                        if L == 1 and (not fixed or 2 <= n <= NH + 1):
                            empty(n - 2, (j - 2) % U, 3, 2 * step + (j - 2) // GH)
                        if L == 3 and (not fixed or 1 <= n <= NH):
                            empty(n - 1, (j - 1) % U, 1, 2 * step + (j - 1) // GH)
                        if not fixed or n < NH:
                            add(n, j, L, 2 * step + j // RR + 1)
                        if j % GH == 0 and L == 1 and (not fixed or 4 <= n <= NH):
                            invert(2 * step + j // GH - 1, (j // GH - 1) % 2)
                        if j % GH == 1 and L == 1 and (not fixed or 9 <= n):
                            scale(2 * step + j // GH - 2, j // GH, step - 1)

                for step in range(2):
                    for j in range(U):
                        head(step, j)
                with dve.Fori(2, NH // U) as step:
                    for j in range(U):
                        head(step, j)
                for j in range(GH + 2):
                    head(NH // U, j)

            @block.scalar
            def _(act):
                def exp(n, j, L, G):
                    t = TT * n + L
                    act.wait_ge(added, t + 1)
                    later(act, turned, t - 2 * TT + 1)
                    if L == 0 and j % GH == 0:
                        later(act, inverted, G - 1)
                    nc.scalar.activation(e[:, j % 2, L, :], neg[:, L, :], ACT.Exp, bias=low[:, j % 2, L:L + 1], scale=-1.0,
                                         accum_out=total[:, j // GH, L, j % GH:j % GH + 1]).then_inc(exped, 1)

                def empty(n, j, L, G):
                    act.wait_ge(turned, TT * n + L + 1)
                    later(act, weighed, TT * (G - 1))
                    nc.scalar.activation(eT[:, j // GH, j % GH, :, L, :], p_t[L][:], ACT.Copy).then_inc(even_out, 1)

                def empty_wide(G):
                    act.wait_ge(wide_turned, G + 1)
                    later(act, ctx_done, G)
                    nc.scalar.activation(wideT[:], p_i[:], ACT.Copy).then_inc(wide_out, 1)

                def head(step, j):
                    n = U * step + j
                    fixed = isinstance(n, int)
                    for L in range(TT):
                        if L == 0 and (not fixed or 2 <= n <= NH + 1):
                            empty(n - 2, (j - 2) % U, 2, 2 * step + (j - 2) // GH)
                        if L == 2 and (not fixed or 1 <= n <= NH):
                            empty(n - 1, (j - 1) % U, 0, 2 * step + (j - 1) // GH)
                        if not fixed or n < NH:
                            exp(n, j, L, 2 * step + j // GH)
                        if j % GH == 3 and L == 1 and (not fixed or 7 <= n):
                            empty_wide(2 * step + j // GH - 1)

                for step in range(2):
                    for j in range(U):
                        head(step, j)
                with act.Fori(2, NH // U) as step:
                    for j in range(U):
                        head(step, j)
                for j in range(GH):
                    head(NH // U, j)


def experts(nc, ins, mod_d, h_d, cT_d, out, nb=NB):
    ctx = ExitStack()
    with ctx:
        def sb(name, shape, dt=F32):
            return ctx.enter_context(nc.sbuf_tensor(name, shape, dt))

        def ps(name, shape):
            return ctx.enter_context(nc.psum_tensor(name, shape, F32))

        def sem(name):
            return ctx.enter_context(nc.semaphore(name))

        EP = NE // 2
        ident = sb("e_ident", [P, P])
        wo = sb("e_wo", [P, KC, E])
        bo = sb("e_bo", [P, E])
        wr = sb("e_wr", [P, KC, NE])
        br = sb("e_br", [P, NE])
        we = sb("e_we", [P, KC, NE * E])
        be = sb("e_be", [NE, E])
        number = sb("e_number", [P, NE])
        h = sb("e_h", [P, 2, TT, E])
        x = sb("e_x", [P, 2, TT, E])
        md = sb("e_mod", [P, 2, 4, E])
        gb = sb("e_gb", [P, 2, E])
        cT = sb("e_cT", [P, 2, KC, S])
        hb = sb("e_hb", [P, 2, TT, E])
        xb = sb("e_xb", [P, 2, TT, E])
        a = sb("e_a", [P, TT, E])
        st = sb("e_stats", [P, TT, 6])
        mv = sb("e_mv", [P, TT, 2])
        var = sb("e_var", [P, TT])
        root = sb("e_root", [P, TT])
        inv = sb("e_inv", [P, TT])
        tmp = sb("e_tmp", [P, TT])
        an = sb("e_an", [P, TT, E])
        x1 = sb("e_x1", [P, 2, TT, E])
        xn = sb("e_xn", [P, TT, E])
        h2 = sb("e_h2", [P, TT, E])
        h2T = sb("e_h2T", [P, 2, KC, S])
        lg = sb("e_logits", [P, TT, NE])
        best = sb("e_best", [P, TT, NE])
        at = sb("e_at", [P, TT, NE], U32)
        atf = sb("e_atf", [P, TT, NE])
        first = sb("e_first", [P, TT, NE])
        second = sb("e_second", [P, TT, NE])
        mask = sb("e_mask", [P, 2, TT, NE])
        mT = sb("e_maskT", [NE, TT, P])
        even = sb("e_even", [P, 2, TT, E])
        odd = sb("e_odd", [P, 2, TT, E])
        y = sb("e_y", [P, 2, TT, E])
        pT = ps("e_pT", [P, KC, S])
        pA = ps("e_pA", [P, TT, E])
        pX = [ps(f"e_pX{i}", [P, 2, E]) for i in range(EP)]
        pR = pT[:, 0, 0:TT * NE].rearrange("p (t e) -> p t e", t=TT)
        pM = pT[0:NE, 1, :].rearrange("e (t p) -> e t p", t=TT)

        ident_zero = sem("e_ident_zero")
        ident_done = sem("e_ident_done")
        w_loaded = sem("e_w_loaded")
        NW = 16 * 7
        ctx_loaded = [sem(f"e_ctx_loaded{u}") for u in range(2)]
        in_loaded = [sem(f"e_in_loaded{u}") for u in range(2)]
        gb_loaded = [sem(f"e_gb_loaded{u}") for u in range(2)]
        attn_done = sem("e_attn_done")
        sums_done = sem("e_sums_done")
        a_done = sem("e_a_done")
        step = sem("e_step")
        root_in = sem("e_root_in")
        root_out = sem("e_root_out")
        an_done = sem("e_an_done")
        x1_step = sem("e_x1_step")
        x1_done = sem("e_x1_done")
        xn_done = sem("e_xn_done")
        h2_step = sem("e_h2_step")
        h2_done = sem("e_h2_done")
        h2_turned = sem("e_h2_turned")
        h2T_out = sem("e_h2T_out")
        routed = sem("e_routed")
        r_step = sem("e_r_step")
        mask_done = sem("e_mask_done")
        mask_turned = sem("e_mask_turned")
        mT_out = sem("e_mT_out")
        bias_done = sem("e_bias_done")
        bias_out = sem("e_bias_out")
        x_unit = sem("e_x_unit")
        even_step = sem("e_even_step")
        odd_step = sem("e_odd_step")
        y_step = sem("e_y_step")
        y_done = sem("e_y_done")
        y_stored = [sem(f"e_y_stored{u}") for u in range(2)]

        x_v = ins["x"].rearrange("b (t p) e -> b p t e", p=P)
        h_v = h_d.rearrange("b (t p) e -> b p t e", p=P)
        out_v = out.rearrange("b (t p) e -> b p t e", p=P)

        def batches(engine, before, each, after):
            before()
            for u in range(2):
                each(0, u)
            with engine.Fori(1, nb // 2 - 1) as pair:
                for u in range(2):
                    each(pair, u)
            each(nb // 2 - 1, 0)
            after()

        with nc.Block() as block:
            @block.sync
            def _(sp):
                def load(pair, u):
                    b = 2 * pair + u
                    later(sp, attn_done, b - 1)
                    sp.dma_start(cT[:, u], cT_d[b].rearrange("(k p) l -> p k l", p=P)).then_inc(ctx_loaded[u], 16)
                    later(sp, sums_done, 2 * (b - 1))
                    sp.dma_start(h[:, u], h_v[b]).then_inc(in_loaded[u], 16)
                    sp.dma_start(x[:, u], x_v[b]).then_inc(in_loaded[u], 16)
                    later(sp, h2_done, b - 1)
                    sp.dma_start(md[:, u], mod_d[b, GAG:CB1 + 1, :].partition_broadcast(P)).then_inc(in_loaded[u], 16)

                def load_gate(pair, u):
                    b = 2 * pair + u
                    later(sp, y_done, b - 1)
                    sp.dma_start(gb[:, u], mod_d[b, GB_, :].partition_broadcast(P)).then_inc(gb_loaded[u], 16)

                sp.dma_start(wo[:], ins["wo"].rearrange("(k p) n -> p k n", p=P)).then_inc(w_loaded, 16)
                sp.dma_start(bo[:], ins["bo"].partition_broadcast(P)).then_inc(w_loaded, 16)
                load(0, 0)
                sp.dma_start(wr[:], ins["wr"].rearrange("(k p) n -> p k n", p=P)).then_inc(w_loaded, 16)
                sp.dma_start(br[:], ins["br"].partition_broadcast(P)).then_inc(w_loaded, 16)
                sp.dma_start(be[:], ins["be"]).then_inc(w_loaded, 16)
                for k in range(KC):
                    sp.dma_start(we[:, k, :], ins["we"][k * P:(k + 1) * P, :]).then_inc(w_loaded, 16)
                load(0, 1)
                load_gate(0, 0)
                load_gate(0, 1)
                with sp.Fori(1, nb // 2) as pair:
                    for u in range(2):
                        load(pair, u)
                        load_gate(pair, u)

            @block.gpsimd
            def _(pool):
                nc.gpsimd.memset(ident[:], 0.0).then_inc(ident_zero, 1)
                pool.wait_ge(ident_zero, 1)
                nc.gpsimd.affine_select(out=ident[:], in_=ident[:], compare_op=ALU.not_equal, fill=1.0,
                                        base=0, pattern=[[-1, P]], channel_multiplier=1).then_inc(ident_done, 1)
                pool.wait_ge(w_loaded, NW)

                def row(t, u, i):
                    return t[:, u, i:i + 1, :].to_broadcast([P, TT, E])

                def sums(pair, u):
                    b = 2 * pair + u
                    pool.wait_ge(in_loaded[u], 48 * (pair + 1))
                    later(pool, a_done, b - 1)
                    later(pool, x1_done, b - 1)
                    nc.gpsimd.tensor_tensor(hb[:, u], h[:, u], bo[:].unsqueeze(1).to_broadcast([P, TT, E]), ALU.add
                                            ).then_inc(sums_done, 1)
                    nc.gpsimd.tensor_tensor(xb[:, u], x[:, u], row(md, u, 1), ALU.add).then_inc(sums_done, 1)

                def residual(pair, u):
                    b = 2 * pair + u
                    pool.wait_ge(an_done, b + 1)
                    pool.wait_ge(sums_done, 2 * (b + 1))
                    later(pool, y_done, b - 1)
                    nc.gpsimd.tensor_tensor(x1[:, u], an[:], row(md, u, 0), ALU.mult).then_inc(x1_step, 1)
                    pool.wait_ge(x1_step, b + 1)
                    nc.gpsimd.tensor_tensor(x1[:, u], x1[:, u], xb[:, u], ALU.add).then_inc(x1_done, 1)

                def modulate(pair, u):
                    b = 2 * pair + u
                    pool.wait_ge(xn_done, b + 1)
                    later(pool, h2_turned, b)
                    nc.gpsimd.tensor_tensor(h2[:], xn[:], row(md, u, 3), ALU.mult).then_inc(h2_step, 1)
                    pool.wait_ge(h2_step, b + 1)
                    nc.gpsimd.tensor_tensor(h2[:], h2[:], row(md, u, 2), ALU.add).then_inc(h2_done, 1)

                def finish(pair, u):
                    b = 2 * pair + u
                    pool.wait_ge(even_step, TT * EP * (b + 1))
                    pool.wait_ge(odd_step, TT * EP * (b + 1))
                    pool.wait_ge(gb_loaded[u], 16 * (pair + 1))
                    later(pool, y_stored[u], 16 * pair)
                    nc.gpsimd.tensor_tensor(y[:, u], even[:, u], odd[:, u], ALU.add).then_inc(y_step, 1)
                    pool.wait_ge(y_step, 2 * b + 1)
                    nc.gpsimd.tensor_tensor(y[:, u], y[:, u], gb[:, u:u + 1, :].to_broadcast([P, TT, E]), ALU.mult
                                            ).then_inc(y_step, 1)
                    pool.wait_ge(y_step, 2 * b + 2)
                    nc.gpsimd.tensor_tensor(y[:, u], y[:, u], x1[:, u], ALU.add).then_inc(y_done, 1)
                    pool.wait_ge(y_done, b + 1)
                    pool.dma_start(out_v[b], y[:, u]).then_inc(y_stored[u], 16)

                def before():
                    sums(0, 0)
                    residual(0, 0)
                    modulate(0, 0)
                    sums(0, 1)

                def each(pair, u):
                    nxt = (pair, 1) if u == 0 else (pair + 1, 0)
                    residual(*nxt)
                    modulate(*nxt)
                    if not isinstance(pair, int) or 2 * pair + u + 2 < nb:
                        sums(pair + 1, u)
                    finish(pair, u)

                batches(pool, before, each, lambda: finish(nb // 2 - 1, 1))
                for u in range(2):
                    pool.wait_ge(y_stored[u], 16 * (nb // 2))

            @block.tensor
            def _(pe):
                pe.wait_ge(ident_done, 1)
                pe.wait_ge(w_loaded, NW)

                def project(pair, u):
                    b = 2 * pair + u
                    pe.wait_ge(ctx_loaded[u], 16 * (pair + 1))
                    later(pe, bias_out, b)
                    for t in range(TT):
                        for k in range(KC):
                            last = nc.tensor.matmul(pA[:, t, :], cT[:, u, k, t * P:(t + 1) * P], wo[:, k, :],
                                                    start=(k == 0), stop=(k == KC - 1))
                    last.then_inc(attn_done, 1)

                def turn_h2(pair, u):
                    pe.wait_ge(h2_done, 2 * pair + u + 1)
                    later(pe, mT_out, 2 * pair + u)
                    for t in range(TT):
                        for c in range(KC):
                            last = nc.tensor.transpose(pT[:, c, t * P:(t + 1) * P], h2[:, t, c * P:(c + 1) * P], ident[:])
                    last.then_inc(h2_turned, 1)

                def route(pair, u):
                    pe.wait_ge(h2T_out, 2 * pair + u + 1)
                    for t in range(TT):
                        for k in range(KC):
                            last = nc.tensor.matmul(pR[:, t, :], h2T[:, u, k, t * P:(t + 1) * P], wr[:, k, :],
                                                    start=(k == 0), stop=(k == KC - 1))
                    last.then_inc(routed, 1)

                def biases(pair, u):
                    b = 2 * pair + u
                    pe.wait_ge(mask_done, b + 1)
                    for t in range(TT):
                        last = nc.tensor.transpose(pM[:, t, :], mask[:, u, t, :], ident[:])
                    last.then_inc(mask_turned, 1)
                    pe.wait_ge(mT_out, b + 1)
                    pe.wait_ge(a_done, b + 1)
                    for t in range(TT):
                        last = nc.tensor.matmul(pA[:, t, :], mT[:, t, :], be[:], start=True, stop=True)
                    last.then_inc(bias_done, 1)

                def expert(pair, u, t):
                    b = 2 * pair + u
                    for n in range(EP):
                        later(pe, even_step, EP * (TT * b + t - 1) + n + 1)
                        later(pe, odd_step, EP * (TT * b + t - 1) + n + 1)
                        for k in range(KC):
                            last = nc.tensor.matmul(pX[n][:], h2T[:, u, k, t * P:(t + 1) * P],
                                                    we[:, k, n * 2 * E:(n + 1) * 2 * E], start=(k == 0), stop=(k == KC - 1))
                        last.then_inc(x_unit, 1)

                def before():
                    project(0, 0)
                    turn_h2(0, 0)
                    route(0, 0)
                    biases(0, 0)

                def each(pair, u):
                    nxt = (pair, 1) if u == 0 else (pair + 1, 0)
                    expert(pair, u, 0)
                    project(*nxt)
                    expert(pair, u, 1)
                    expert(pair, u, 2)
                    turn_h2(*nxt)
                    route(*nxt)
                    expert(pair, u, 3)
                    biases(*nxt)

                def after():
                    for t in range(TT):
                        expert(nb // 2 - 1, 1, t)

                batches(pe, before, each, after)

            @block.scalar
            def _(act):
                def prepare(pair, u):
                    b = 2 * pair + u
                    for i in range(2):
                        act.wait_ge(root_in, 2 * b + i + 1)
                        nc.scalar.activation(root[:], var[:], ACT.Sqrt).then_inc(root_out, 1)
                    act.wait_ge(h2_turned, b + 1)
                    later(act, x_unit, TT * EP * (b - 1))
                    nc.scalar.activation(h2T[:, u], pT[:], ACT.Copy).then_inc(h2T_out, 1)
                    act.wait_ge(mask_turned, b + 1)
                    later(act, bias_done, b)
                    nc.scalar.activation(mT[:], pM, ACT.Copy).then_inc(mT_out, 1)
                    act.wait_ge(bias_done, b + 1)
                    later(act, y_step, 2 * (b - 2) + 1)
                    nc.scalar.activation(even[:, u], pA[:], ACT.Copy).then_inc(bias_out, 1)

                batches(act, lambda: prepare(0, 0),
                        lambda pair, u: prepare(*((pair, 1) if u == 0 else (pair + 1, 0))), lambda: None)

            @block.vector
            def _(dve):
                NSTEP = 7
                for e in range(NE):
                    last = nc.vector.memset(number[:, e:e + 1], float(e))
                last.then_inc(r_step, 1)
                dve.wait_ge(w_loaded, NW)

                def normalise(src, dst, eps, b, i, free):
                    count = [0]

                    def then(instruction):
                        count[0] += 1
                        instruction.then_inc(step, 1)
                        dve.wait_ge(step, NSTEP * (2 * b + i) + count[0])

                    def root_of():
                        dve.wait_ge(root_out, 2 * b + i + 1)

                    for t in range(TT):
                        last = nc.vector.bn_stats(st[:, t, :], src[:, t, :])
                    then(last)
                    nc.vector.memset(tmp[:], 0.0)
                    for t in range(TT):
                        last = nc.vector.bn_aggr(mv[:, t, :], st[:, t, :])
                    then(last)
                    nc.vector.tensor_scalar_add(var[:], mv[:, :, 1], eps).then_inc(root_in, 1)
                    inverse_root(nc, then, inv[:], var[:], root_of, root[:], tmp[:])
                    free()
                    for t in range(TT):
                        last = nc.vector.tensor_scalar(dst[:, t, :], src[:, t, :], mv[:, t, 0:1], inv[:, t:t + 1],
                                                       ALU.subtract, ALU.mult)
                    assert count[0] == NSTEP
                    return last

                def attn_norm(pair, u):
                    b = 2 * pair + u
                    dve.wait_ge(attn_done, b + 1)
                    dve.wait_ge(sums_done, 2 * b + 1)
                    later(dve, an_done, b)
                    nc.vector.tensor_tensor(a[:], pA[:], hb[:, u], ALU.add).then_inc(a_done, 1)
                    dve.wait_ge(a_done, b + 1)
                    normalise(a, an, EPS_ATTN, b, 0, lambda: later(dve, x1_step, b)).then_inc(an_done, 1)

                def x1_norm(pair, u):
                    b = 2 * pair + u
                    dve.wait_ge(x1_done, b + 1)
                    dve.wait_ge(an_done, b + 1)
                    normalise(x1[:, u], xn, EPS_LN, b, 1, lambda: later(dve, h2_step, b)).then_inc(xn_done, 1)

                def route(pair, u):
                    b = 2 * pair + u
                    count = [0]

                    def then(instruction):
                        count[0] += 1
                        instruction.then_inc(r_step, 1)
                        dve.wait_ge(r_step, 1 + 7 * b + count[0])

                    dve.wait_ge(routed, b + 1)
                    then(nc.vector.tensor_tensor(lg[:], pR, br[:].unsqueeze(1).to_broadcast([P, TT, NE]), ALU.add))
                    nc.vector.memset(tmp[:], 0.0)
                    for t in range(TT):
                        last = nc.vector.max(best[:, t, :], lg[:, t, :])
                    then(last)
                    nc.vector.memset(tmp[:], 0.0)
                    for t in range(TT):
                        last = nc.vector.max_index(at[:, t, :], best[:, t, :], lg[:, t, :])
                    then(last)
                    then(nc.vector.tensor_copy(atf[:], at[:]))
                    num = number[:].unsqueeze(1).to_broadcast([P, TT, NE])
                    then(nc.vector.tensor_tensor(first[:], num, atf[:, :, 0:1].to_broadcast([P, TT, NE]), ALU.is_equal))
                    then(nc.vector.tensor_tensor(second[:], num, atf[:, :, 1:2].to_broadcast([P, TT, NE]), ALU.is_equal))
                    then(nc.vector.tensor_tensor(mask[:, u], first[:], second[:], ALU.add))
                    dve.sem_inc(mask_done, 1)

                def combine(pair, u, t):
                    b = 2 * pair + u
                    if t == 0:
                        dve.wait_ge(bias_out, b + 1)
                        later(dve, y_step, 2 * (b - 2) + 1)
                    for n in range(EP):
                        unit = EP * (TT * b + t) + n
                        dve.wait_ge(x_unit, unit + 1)
                        m = mask[:, u, t, :]
                        if n:
                            dve.wait_ge(even_step, unit)
                        nc.vector.scalar_tensor_tensor(even[:, u, t, :], pX[n][:, 0, :], m[:, 2 * n:2 * n + 1],
                                                       even[:, u, t, :], ALU.mult, ALU.add).then_inc(even_step, 1)
                        if n:
                            dve.wait_ge(odd_step, unit)
                            nc.vector.scalar_tensor_tensor(odd[:, u, t, :], pX[n][:, 1, :], m[:, 2 * n + 1:2 * n + 2],
                                                           odd[:, u, t, :], ALU.mult, ALU.add).then_inc(odd_step, 1)
                        else:
                            nc.vector.tensor_scalar(odd[:, u, t, :], pX[n][:, 1, :], m[:, 1:2], None, ALU.mult
                                                    ).then_inc(odd_step, 1)

                def before():
                    attn_norm(0, 0)
                    x1_norm(0, 0)
                    route(0, 0)

                def each(pair, u):
                    nxt = (pair, 1) if u == 0 else (pair + 1, 0)
                    combine(pair, u, 0)
                    attn_norm(*nxt)
                    combine(pair, u, 1)
                    x1_norm(*nxt)
                    combine(pair, u, 2)
                    route(*nxt)
                    combine(pair, u, 3)

                def after():
                    for t in range(TT):
                        combine(nb // 2 - 1, 1, t)

                batches(dve, before, each, after)


def program(nc, ins, out):
    def scratch(name, shape, dt=F32):
        return nc.dram_tensor(name, shape, dt, kind="Internal").ap()

    mod_d = scratch("mod_scratch", [NB, NMOD, E])
    tab_d = scratch("table_scratch", [ROWS, TAB], BF16)
    h_d = scratch("h_scratch", [NB, S, E])
    v_d = scratch("v_scratch", [NB, P, H, TT, D])
    qs_d = scratch("q_chunks_scratch", [NG, LC, GB, SD, H, LW], BF16)
    ks_d = scratch("k_chunks_scratch", [NG, RC, GB, SD, H, RW], BF16)
    qf_d = scratch("q_rows_scratch", [NG, 1, GB, SD, H, S], BF16)
    cT_d = scratch("ctx_scratch", [NB, E, S])
    r_d = [scratch(f"r{g}_scratch", [P * RPITCH]).rearrange("(n q) -> n q", q=RPITCH)[:, 0:S * S]
           .rearrange("n (l r) -> n l r", r=S) for g in range(NG)]
    modulation(nc, ins, mod_d, tab_d)
    projections(nc, ins, mod_d, h_d, qs_d, ks_d, qf_d, v_d)
    distances(nc, tab_d, qs_d, ks_d, r_d)
    attention(nc, qf_d, ks_d, v_d, r_d, cT_d)
    experts(nc, ins, mod_d, h_d, cT_d, out)


def kernel(**inputs):
    import numpy as np
    import concourse.bacc as bacc
    from concourse.bass_utils import run_bass_kernel_spmd

    a = {n: np.asarray(v) for n, v in inputs.items()}

    def attn(name):
        return a["L0_attn_" + name]

    def by_d(w):
        return w.reshape(-1, H, D).transpose(0, 2, 1).reshape(-1, E)

    arrays = {
        "x": attn("hidden_states"), "cT": a["L0_c"].T, "wmod": a["L0_wmod"], "eT": attn("dist_emb").T,
        "gamma": attn("ln_gamma"), "beta": attn("ln_beta"),
        "wq": by_d(attn("Wq")), "wk": by_d(attn("Wk")),
        "bq": by_d(attn("bq")).reshape(KC, P).T, "bk": by_d(attn("bk")).reshape(KC, P).T,
        "wv": attn("Wv"), "bv": attn("bv"), "wo": attn("Wo"), "bo": attn("bo"),
        "wr": a["L0_ffn_w_router"].T, "br": a["L0_ffn_b_router"],
        "we": a["L0_ffn_w_experts"].transpose(2, 0, 1).reshape(E, NE * E), "be": a["L0_ffn_b_experts"],
    }
    nc = bacc.Bacc("TRN2", target_bir_lowering=False, num_devices=1)
    maps, ins = {}, {}
    for name, array in arrays.items():
        array = np.ascontiguousarray(array)
        maps["in_" + name] = array
        ins[name] = nc.dram_tensor("in_" + name, array.shape, mybir.dt.from_np(array.dtype), kind="ExternalInput").ap()
    out = nc.dram_tensor("out_x", (NB, S, E), F32, kind="ExternalOutput").ap()
    program(nc, ins, out)
    return run_bass_kernel_spmd(nc, [maps], core_ids=[0]).results[0]["out_x"]
```

```python
from contextlib import ExitStack

import concourse.bass as bass
from concourse import mybir

F32 = mybir.dt.float32
BF16 = mybir.dt.bfloat16
U32 = mybir.dt.uint32
ALU = mybir.AluOpType
ACT = mybir.ActivationFunctionType

P = 128
NB, S, E = 16, 512, 256
H = 16
D = E // H
M = 256
KC = E // P
TT = S // P
NE = 8
EPS_LN = 1e-5
EPS_ATTN = 1e-12

A_PARTS = (0, 1, 2, 0, 1, 0)
B_PARTS = (0, 0, 0, 1, 1, 2)
ROWS = len(A_PARTS) * D
SD = 3 * D

GB = P // H
NG = NB // GB
LW, RW = 64, 128
LC, RC = S // LW, S // RW
TAB = 2 * S
WIN = LW + RW
RPITCH = S * S + 1024

SA, CA1, GAG, GAB, SB, CB1, GB_ = range(7)
NMOD = 7


def later(engine, semaphore, value):
    if isinstance(value, int) and value <= 0:
        return
    engine.wait_ge(semaphore, value)


def rows_of(parts):
    runs, at = [], 0
    while at < len(parts):
        n = 1
        while at + n < len(parts) and parts[at + n] == parts[at] + n:
            n += 1
        runs.append((at * D, parts[at] * D, n * D))
        at += n
    return runs


A_RUNS, B_RUNS = rows_of(A_PARTS), rows_of(B_PARTS)


def modulation(nc, ins, mod_d, tab_d):
    ctx = ExitStack()
    with ctx:
        def sb(name, shape, dt=F32):
            return ctx.enter_context(nc.sbuf_tensor(name, shape, dt))

        def sem(name):
            return ctx.enter_context(nc.semaphore(name))

        cT = sb("m_cT", [P, KC, NB])
        en = sb("m_en", [P, KC, NB])
        den = sb("m_den", [P, KC, NB])
        rec = sb("m_rec", [P, KC, NB])
        act = sb("m_silu", [P, KC, NB])
        wmod = sb("m_wmod", [P, KC, 6 * E])
        gamma = sb("m_gamma", [NB, E])
        beta = sb("m_beta", [NB, E])
        up = sb("m_up", [NB, 2, E])
        dn = sb("m_dn", [NB, 2, E])
        pos = sb("m_pos", [NB, 2, E])
        neg = sb("m_neg", [NB, 2, E])
        gate = sb("m_gate", [NB, 2, E])
        mod = sb("m_mod", [NB, NMOD, E])
        eT = sb("m_eT", [D, 2 * M])
        t32 = sb("m_t32", [D, TAB])
        res = sb("m_res", [D, TAB])
        res2 = sb("m_res2", [D, TAB])
        parts = sb("m_parts", [D, 3, TAB], BF16)
        pm = ctx.enter_context(nc.psum_tensor("m_psum", [NB, 3, 512], F32))

        loaded = sem("m_loaded")
        e_loaded = sem("m_e_loaded")
        exp_done = sem("m_exp_done")
        silu_done = sem("m_silu_done")
        mod_product = sem("m_mod_product")
        step = sem("m_step")
        t_step = sem("m_t_step")
        mod_done = sem("m_mod_done")
        table_done = sem("m_table_done")
        stored = sem("m_stored")

        with nc.Block() as block:
            @block.sync
            def _(sp):
                sp.dma_start(cT[:], ins["cT"].rearrange("(k p) b -> p k b", p=P)).then_inc(loaded, 16)
                sp.dma_start(eT[:, 0:2 * M - 1], ins["eT"]).then_inc(e_loaded, 16)
                sp.dma_start(wmod[:], ins["wmod"].rearrange("(k p) n -> p k n", p=P)).then_inc(loaded, 16)
                sp.dma_start(gamma[:], ins["gamma"].partition_broadcast(NB)).then_inc(loaded, 16)
                sp.dma_start(beta[:], ins["beta"].partition_broadcast(NB)).then_inc(loaded, 16)
                sp.wait_ge(table_done, 1)
                for row, part in enumerate(B_PARTS):
                    sp.dma_start(tab_d[row * D:(row + 1) * D, :], parts[:, part, :]).then_inc(stored, 16)
                sp.wait_ge(mod_done, 1)
                sp.dma_start(mod_d[:, :, :], mod[:]).then_inc(stored, 16)
                sp.wait_ge(stored, 16 * (len(B_PARTS) + 1))

            @block.scalar
            def _(act_e):
                act_e.wait_ge(loaded, 64)
                nc.scalar.activation(en[:], cT[:], ACT.Exp, scale=-1.0).then_inc(exp_done, 1)

            @block.tensor
            def _(pe):
                pe.wait_ge(silu_done, 1)
                for n in range(3):
                    for k in range(KC):
                        last = nc.tensor.matmul(pm[:, n, :], act[:, k, :], wmod[:, k, n * 512:(n + 1) * 512],
                                                start=(k == 0), stop=(k == KC - 1))
                last.then_inc(mod_product, 1)

            @block.vector
            def _(dve):
                done = [0, 0]

                def then(instruction):
                    done[0] += 1
                    instruction.then_inc(step, 1)
                    dve.wait_ge(step, done[0])

                def then_t(instruction):
                    done[1] += 1
                    instruction.then_inc(t_step, 1)
                    dve.wait_ge(t_step, done[1])

                dve.wait_ge(exp_done, 1)
                then(nc.vector.tensor_scalar_add(den[:], en[:], 1.0))
                then(nc.vector.reciprocal(rec[:], den[:]))
                nc.vector.tensor_tensor(act[:], cT[:], rec[:], ALU.mult).then_inc(silu_done, 1)
                dve.wait_ge(e_loaded, 16)
                nc.vector.tensor_copy(t32[:, 0:M], eT[:, M - 1:2 * M - 1])
                nc.vector.tensor_copy(t32[:, M:3 * M - 1], eT[:, 0:2 * M - 1])
                then_t(nc.vector.tensor_copy(t32[:, 3 * M - 1:TAB], eT[:, 2 * M - 2:2 * M - 1].to_broadcast([D, TAB - 3 * M + 1])))
                then_t(nc.vector.tensor_copy(parts[:, 0, :], t32[:]))
                then_t(nc.vector.tensor_tensor(res[:], t32[:], parts[:, 0, :], ALU.subtract))
                then_t(nc.vector.tensor_copy(parts[:, 1, :], res[:]))
                nc.vector.tensor_tensor(parts[:, 2, :], res[:], parts[:, 1, :], ALU.subtract).then_inc(table_done, 1)
                dve.wait_ge(mod_product, 1)
                m6 = pm[:, :, :].rearrange("b n (a f) -> b (n a) f", a=2)
                nc.vector.tensor_copy(mod[:, SA, :], m6[:, 0, :])
                nc.vector.tensor_copy(mod[:, SB, :], m6[:, 3, :])
                nc.vector.tensor_scalar_add(mod[:, CA1, :], m6[:, 1, :], 1.0)
                nc.vector.tensor_scalar_add(mod[:, CB1, :], m6[:, 4, :], 1.0)
                for i, row in enumerate((2, 5)):
                    nc.vector.tensor_scalar(up[:, i, :], m6[:, row, :], 0.25, None, ALU.max)
                    nc.vector.tensor_scalar(dn[:, i, :], m6[:, row, :], -0.25, None, ALU.min)
                    nc.vector.tensor_scalar(pos[:, i, :], m6[:, row, :], 0.0, None, ALU.is_ge)
                    then(nc.vector.tensor_scalar(neg[:, i, :], m6[:, row, :], 0.0, None, ALU.is_lt))
                then(nc.vector.tensor_tensor(up[:], up[:], pos[:], ALU.mult))
                then(nc.vector.tensor_tensor(dn[:], dn[:], neg[:], ALU.mult))
                then(nc.vector.tensor_tensor(gate[:], up[:], dn[:], ALU.add))
                nc.vector.tensor_copy(mod[:, GB_, :], gate[:, 1, :])
                nc.vector.tensor_tensor(mod[:, GAG, :], gate[:, 0, :], gamma[:], ALU.mult)
                nc.vector.tensor_tensor(mod[:, GAB, :], gate[:, 0, :], beta[:], ALU.mult).then_inc(mod_done, 1)


def inverse_root(nc, then, y, v, root_of, s, t):
    root_of()
    then(nc.vector.reciprocal(y, s))
    then(nc.vector.tensor_tensor(t, y, y, ALU.mult))
    then(nc.vector.tensor_tensor(t, t, v, ALU.mult))
    then(nc.vector.tensor_scalar(t, t, -0.5, 1.5, ALU.mult, ALU.add))
    then(nc.vector.tensor_tensor(y, y, t, ALU.mult))


def projections(nc, ins, mod_d, h_d, qs_d, ks_d, qf_d, v_d, nb=NB):
    ctx = ExitStack()
    with ctx:
        def sb(name, shape, dt=F32):
            return ctx.enter_context(nc.sbuf_tensor(name, shape, dt))

        def ps(name, shape):
            return ctx.enter_context(nc.psum_tensor(name, shape, F32))

        def sem(name):
            return ctx.enter_context(nc.semaphore(name))

        wqk = sb("a_wqk", [P, 2, KC, E])
        wv = sb("a_wv", [P, KC, E])
        bqk = sb("a_bqk", [P, 2, KC])
        bv = sb("a_bv", [P, E])
        ident = sb("a_ident", [P, P])
        x = sb("a_x", [P, 2, TT, E])
        md = sb("a_mod", [P, 2, 2, E])
        st = sb("a_stats", [P, 2, TT, 6])
        mv = sb("a_mv", [P, 2, TT, 2])
        var = sb("a_var", [P, 2, TT])
        root = sb("a_root", [P, 2, TT])
        inv = sb("a_inv", [P, 2, TT])
        tmp = sb("a_tmp", [P, 2, TT])
        xn = sb("a_xn", [P, 2, TT, E])
        h = sb("a_h", [P, 2, TT, E])
        hT = sb("a_hT", [P, 2, KC, S])
        q32 = sb("a_q32", [P, 2, KC, S])
        rest = sb("a_rest", [P, 2, KC, S])
        part = sb("a_part", [P, 2, 2, 3, KC, S], BF16)
        vs = sb("a_v", [P, 2, H, TT, D])
        pT = ps("a_pT", [P, KC, S])
        pQ = ps("a_pQ", [P, 2, KC, S])
        pV = ps("a_pV", [P, TT, E])

        w_loaded = sem("a_w_loaded")
        ident_zero = sem("a_ident_zero")
        ident_done = sem("a_ident_done")
        x_loaded = [sem(f"a_x_loaded{u}") for u in range(2)]
        root_in = sem("a_root_in")
        root_out = sem("a_root_out")
        step = sem("a_step")
        xn_done = sem("a_xn_done")
        h_step = sem("a_h_step")
        h_done = sem("a_h_done")
        tr_done = sem("a_tr_done")
        hT_done = sem("a_hT_done")
        qk_done = sem("a_qk_done")
        v_done = sem("a_v_done")
        q32_done = sem("a_q32_done")
        part0_done = sem("a_part0_done")
        rest_done = sem("a_rest_done")
        part1_done = sem("a_part1_done")
        part2_done = sem("a_part2_done")
        vs_done = sem("a_vs_done")
        h_stored = [sem(f"a_h_stored{u}") for u in range(2)]
        q_stored = [sem(f"a_q_stored{u}") for u in range(2)]
        v_stored = [sem(f"a_v_stored{u}") for u in range(2)]

        x_v = ins["x"].rearrange("b (t p) e -> b p t e", p=P)
        h_v = h_d.rearrange("b (t p) e -> b p t e", p=P)

        with nc.Block() as block:
            @block.sync
            def _(sp):
                for i, name in enumerate(("wq", "wk")):
                    sp.dma_start(wqk[:, i], ins[name].rearrange("(k p) n -> p k n", p=P)).then_inc(w_loaded, 16)
                    sp.dma_start(bqk[:, i], ins["b" + name[1]]).then_inc(w_loaded, 16)
                sp.dma_start(wv[:], ins["wv"].rearrange("(k p) n -> p k n", p=P)).then_inc(w_loaded, 16)
                sp.dma_start(bv[:], ins["bv"].partition_broadcast(P)).then_inc(w_loaded, 16)

                def store(pair, u):
                    b = 2 * pair + u
                    g, b8 = b // GB, b % GB
                    sp.wait_ge(h_done, b + 1)
                    sp.dma_start(h_v[b], h[:, u]).then_inc(h_stored[u], 16)
                    sp.wait_ge(vs_done, b + 1)
                    sp.dma_start(v_d[b], vs[:, u].rearrange("p h t d -> p (h t d)")).then_inc(v_stored[u], 16)
                    for i, dsts in enumerate((((qs_d, LW), (qf_d, S)), ((ks_d, RW),))):
                        sp.wait_ge(part0_done, 2 * b + i + 1)
                        sp.wait_ge(part1_done, 2 * b + i + 1)
                        sp.wait_ge(part2_done, 2 * b + i + 1)
                        for (dst, w), s, c in ((dw, s, c) for dw in dsts for s in range(3) for c in range(KC)):
                                to = dst[g, :, b8, s * D + c * (D // KC):s * D + (c + 1) * (D // KC), :, :]
                                sp.dma_start(to.rearrange("n d h w -> (d h) n w"),
                                             part[:, u, i, s, c, :].rearrange("p (n w) -> p n w", w=w)
                                             ).then_inc(q_stored[u], 16)

                with sp.Fori(0, nb // 2) as pair:
                    for u in range(2):
                        store(pair, u)
                for u in range(2):
                    sp.wait_ge(h_stored[u], 16 * (nb // 2))
                    sp.wait_ge(v_stored[u], 16 * (nb // 2))
                    sp.wait_ge(q_stored[u], 16 * 18 * (nb // 2))

            @block.gpsimd
            def _(pool):
                def load(pair, u):
                    b = 2 * pair + u
                    later(pool, h_done, b - 1)
                    pool.dma_start(x[:, u], x_v[b]).then_inc(x_loaded[u], 16)
                    pool.dma_start(md[:, u], mod_d[b, SA:CA1 + 1, :].partition_broadcast(P)).then_inc(x_loaded[u], 16)

                load(0, 0)
                load(0, 1)
                nc.gpsimd.memset(ident[:], 0.0).then_inc(ident_zero, 1)
                pool.wait_ge(ident_zero, 1)
                nc.gpsimd.affine_select(out=ident[:], in_=ident[:], compare_op=ALU.not_equal, fill=1.0,
                                        base=0, pattern=[[-1, P]], channel_multiplier=1).then_inc(ident_done, 1)

                def modulate(pair, u):
                    b = 2 * pair + u
                    pool.wait_ge(xn_done, b + 1)
                    later(pool, tr_done, b - 1)
                    later(pool, h_stored[u], 16 * pair)
                    nc.gpsimd.tensor_tensor(h[:, u], xn[:, u], md[:, u, 1:2, :].to_broadcast([P, TT, E]),
                                            ALU.mult).then_inc(h_step, 1)
                    pool.wait_ge(h_step, b + 1)
                    nc.gpsimd.tensor_tensor(h[:, u], h[:, u], md[:, u, 0:1, :].to_broadcast([P, TT, E]),
                                            ALU.add).then_inc(h_done, 1)

                for u in range(2):
                    modulate(0, u)
                    load(1, u)
                with pool.Fori(1, nb // 2 - 1) as pair:
                    for u in range(2):
                        modulate(pair, u)
                        load(pair + 1, u)
                for u in range(2):
                    modulate(nb // 2 - 1, u)

            @block.tensor
            def _(pe):
                pe.wait_ge(ident_done, 1)
                pe.wait_ge(w_loaded, 96)

                def turn(pair, u):
                    b = 2 * pair + u
                    pe.wait_ge(h_done, b + 1)
                    later(pe, hT_done, b)
                    for t in range(TT):
                        for c in range(KC):
                            last = nc.tensor.transpose(pT[:, c, t * P:(t + 1) * P], h[:, u, t, c * P:(c + 1) * P],
                                                       ident[:])
                    last.then_inc(tr_done, 1)

                def make_qk(pair, u):
                    b = 2 * pair + u
                    pe.wait_ge(hT_done, b + 1)
                    for i in range(2):
                        later(pe, q32_done, 2 * (b - 1) + i + 1)
                        for c in range(KC):
                            for k in range(KC):
                                last = nc.tensor.matmul(pQ[:, i, c, :], wqk[:, i, k, c * P:(c + 1) * P],
                                                        hT[:, u, k, :], start=(k == 0), stop=(k == KC - 1))
                        last.then_inc(qk_done, 1)

                def make_v(pair, u):
                    b = 2 * pair + u
                    later(pe, vs_done, b)
                    for t in range(TT):
                        for k in range(KC):
                            last = nc.tensor.matmul(pV[:, t, :], hT[:, u, k, t * P:(t + 1) * P], wv[:, k, :],
                                                    start=(k == 0), stop=(k == KC - 1))
                    last.then_inc(v_done, 1)

                def project(pair, u, more=True):
                    make_qk(pair, u)
                    if more:
                        turn(*((pair, 1) if u == 0 else (pair + 1, 0)))
                    make_v(pair, u)

                turn(0, 0)
                for u in range(2):
                    project(0, u)
                with pe.Fori(1, nb // 2 - 1) as pair:
                    for u in range(2):
                        project(pair, u)
                for u in range(2):
                    project(nb // 2 - 1, u, more=(u == 0))

            @block.scalar
            def _(act):
                act.wait_ge(w_loaded, 96)

                def take_root(pair, u):
                    b = 2 * pair + u
                    act.wait_ge(root_in, b + 1)
                    nc.scalar.activation(root[:, u], var[:, u], ACT.Sqrt).then_inc(root_out, 1)

                def empty(pair, u):
                    b = 2 * pair + u
                    act.wait_ge(tr_done, b + 1)
                    later(act, v_done, b - 1)
                    nc.scalar.activation(hT[:, u], pT[:], ACT.Copy).then_inc(hT_done, 1)

                def split(pair, u, more=True, more_roots=True):
                    b = 2 * pair + u
                    for i in range(2):
                        act.wait_ge(qk_done, 2 * b + i + 1)
                        later(act, rest_done, 2 * (b - 1) + i + 1)
                        later(act, part0_done, 2 * (b - 1) + i + 1)
                        for c in range(KC):
                            last = nc.scalar.activation(q32[:, i, c, :], pQ[:, i, c, :], ACT.Identity,
                                                        bias=bqk[:, i, c:c + 1])
                        last.then_inc(q32_done, 1)
                        act.wait_ge(q32_done, 2 * b + i + 1)
                        later(act, q_stored[u], 16 * 18 * pair)
                        nc.scalar.activation(part[:, u, i, 0], q32[:, i], ACT.Copy).then_inc(part0_done, 1)
                    if more:
                        empty(*((pair, 1) if u == 0 else (pair + 1, 0)))
                    for i in range(2):
                        if i == 1 and more_roots:
                            take_root(pair + 1, u)
                        act.wait_ge(rest_done, 2 * b + i + 1)
                        nc.scalar.activation(part[:, u, i, 1], rest[:, i], ACT.Copy).then_inc(part1_done, 1)

                take_root(0, 0)
                take_root(0, 1)
                empty(0, 0)
                for u in range(2):
                    split(0, u)
                with act.Fori(1, nb // 2 - 1) as pair:
                    for u in range(2):
                        split(pair, u)
                for u in range(2):
                    split(nb // 2 - 1, u, more=(u == 0), more_roots=False)

            @block.vector
            def _(dve):
                dve.wait_ge(w_loaded, 96)
                NSTEP = 7

                def normalise(pair, u):
                    b = 2 * pair + u
                    count = [0]

                    def then(instruction):
                        count[0] += 1
                        instruction.then_inc(step, 1)
                        dve.wait_ge(step, NSTEP * b + count[0])

                    def root_of():
                        dve.wait_ge(root_out, b + 1)

                    dve.wait_ge(x_loaded[u], 32 * (pair + 1))
                    for t in range(TT):
                        last = nc.vector.bn_stats(st[:, u, t, :], x[:, u, t, :])
                    then(last)
                    nc.vector.memset(tmp[:, u], 0.0)
                    for t in range(TT):
                        last = nc.vector.bn_aggr(mv[:, u, t, :], st[:, u, t, :])
                    then(last)
                    nc.vector.tensor_scalar_add(var[:, u], mv[:, u, :, 1], EPS_LN).then_inc(root_in, 1)
                    inverse_root(nc, then, inv[:, u], var[:, u], root_of, root[:, u], tmp[:, u])
                    later(dve, h_step, b - 1)
                    for t in range(TT):
                        last = nc.vector.tensor_scalar(xn[:, u, t, :], x[:, u, t, :], mv[:, u, t, 0:1],
                                                       inv[:, u, t:t + 1], ALU.subtract, ALU.mult)
                    last.then_inc(xn_done, 1)
                    assert count[0] == NSTEP

                def split(pair, u, more=True):
                    b = 2 * pair + u
                    for i in range(2):
                        dve.wait_ge(part0_done, 2 * b + i + 1)
                        later(dve, part2_done, 2 * (b - 1) + i + 1)
                        nc.vector.tensor_tensor(rest[:, i], q32[:, i], part[:, u, i, 0], ALU.subtract
                                                ).then_inc(rest_done, 1)
                    if more:
                        normalise(pair + 1, u)
                    dve.wait_ge(v_done, b + 1)
                    later(dve, v_stored[u], 16 * pair)
                    for t in range(TT):
                        last = nc.vector.tensor_tensor(vs[:, u, :, t, :], pV[:, t, :].rearrange("p (h d) -> p h d", d=D),
                                                       bv[:].rearrange("p (h d) -> p h d", d=D), ALU.add)
                    last.then_inc(vs_done, 1)
                    for i in range(2):
                        dve.wait_ge(part1_done, 2 * b + i + 1)
                        nc.vector.tensor_tensor(part[:, u, i, 2], rest[:, i], part[:, u, i, 1], ALU.subtract
                                                ).then_inc(part2_done, 1)

                normalise(0, 0)
                normalise(0, 1)
                for u in range(2):
                    split(0, u)
                with dve.Fori(1, nb // 2 - 1) as pair:
                    for u in range(2):
                        split(pair, u)
                for u in range(2):
                    split(nb // 2 - 1, u, more=False)


def distances(nc, tab_d, qs_d, ks_d, r_d, ng=NG):
    ctx = ExitStack()
    with ctx:
        def sb(name, shape, dt=F32):
            return ctx.enter_context(nc.sbuf_tensor(name, shape, dt))

        def sem(name):
            return ctx.enter_context(nc.semaphore(name))

        UNIT = 1024
        QL = UNIT // RW
        KR = UNIT // LW
        NU = LW * RW // UNIT
        LEAD = 1
        NP = 8
        q = [sb(f"d_q{u}", [ROWS, P, LW], BF16) for u in range(2)]
        k = [sb(f"d_k{u}", [ROWS, P, RW], BF16) for u in range(2)]
        win = [sb(f"d_win{u}", [ROWS, WIN], BF16) for u in range(4)]
        r = [sb(f"d_r{u}", [P, LW, RW]) for u in range(2)]
        pq = [ctx.enter_context(nc.psum_tensor(f"d_pq{u}", [P, QL, RW], F32)) for u in range(2)]
        pk = [ctx.enter_context(nc.psum_tensor(f"d_pk{u}", [P, KR, LW], F32)) for u in range(2)]

        q_loaded = [sem(f"d_q_loaded{u}") for u in range(2)]
        k_loaded = [sem(f"d_k_loaded{u}") for u in range(2)]
        win_loaded = [sem(f"d_win_loaded{u}") for u in range(4)]
        q_units = sem("d_q_units")
        k_units = sem("d_k_units")
        q_out = sem("d_q_out")
        k_added = sem("d_k_added")
        r_stored = [[sem(f"d_r_stored{u}_{p}") for p in range(NP)] for u in range(2)]

        RH = RC // 2
        LCP = LC // 2
        NHALF = ng * RH

        with nc.Block() as block:
            @block.gpsimd
            def _(pool):
                def load_k(half, v):
                    later(pool, k_units, NU * (16 * half - 1 + v))
                    for row, stored, rows in A_RUNS:
                        src = ks_d[half // RH, (half % RH) * 2 + v, :, stored:stored + rows, :, :]
                        pool.dma_start(k[v][row:row + rows, :, :].rearrange("r (b h) w -> r b (h w)", b=GB),
                                       src.rearrange("b r h w -> r b (h w)")).then_inc(k_loaded[v], 16)

                def load_q(half, lcp, u):
                    later(pool, k_units, NU * (16 * half + 4 * lcp + 2 * u - 2))
                    for row, stored, rows in A_RUNS:
                        src = qs_d[half // RH, 2 * lcp + u, :, stored:stored + rows, :, :]
                        pool.dma_start(q[u][row:row + rows, :, :].rearrange("r (b h) w -> r b (h w)", b=GB),
                                       src.rearrange("b r h w -> r b (h w)")).then_inc(q_loaded[u], 16)
                    for v in range(2):
                        col = (2 * lcp + u) * LW - ((half % RH) * 2 + v) * RW + S - RW
                        pool.dma_start(win[2 * u + v][:], tab_d[:, bass.ds(col, WIN)]).then_inc(win_loaded[2 * u + v], 16)

                def body(half):
                    load_q(half, 0, 0)
                    load_k(half, 0)
                    load_k(half, 1)
                    load_q(half, 0, 1)
                    with pool.Fori(1, LCP) as lcp:
                        for u in range(2):
                            load_q(half, lcp, u)

                body(0)
                with pool.Fori(1, NHALF) as half:
                    body(half)

            @block.tensor
            def _(pe):
                def q_unit(at, j, n):
                    u, v = j // 2, j % 2
                    if n == 0:
                        pe.wait_ge(q_loaded[u], 16 * len(A_RUNS) * (at + 1))
                        pe.wait_ge(win_loaded[j], 16 * (at + 1))
                    later(pe, q_out, NU * (4 * at + j) + n - 1)
                    for a in range(QL):
                        l = n * QL + a
                        rhs = bass.AP(win[j], l + RW - 1, [[WIN, ROWS], [-1, RW]])
                        last = nc.tensor.matmul(pq[n % 2][:, a, :], q[u][:, :, l], rhs, start=True, stop=True)
                    last.then_inc(q_units, 1)

                def k_unit(at, j, n):
                    v = j % 2
                    if n == 0:
                        pe.wait_ge(k_loaded[v], 16 * len(A_RUNS) * (at // LCP + 1))
                    later(pe, k_added, NU * (4 * at + j) + n - 1)
                    for a in range(KR):
                        c = n * KR + a
                        last = nc.tensor.matmul(pk[n % 2][:, a, :], k[v][:, :, c],
                                                win[j][:, RW - 1 - c:RW - 1 - c + LW], start=True, stop=True)
                    last.then_inc(k_units, 1)

                def chunk(at, j, more=True):
                    for n in range(NU + LEAD):
                        if n < NU:
                            k_unit(at, j, n)
                        if n >= LEAD and more:
                            q_unit(at + (j + 1) // 4, (j + 1) % 4, n - LEAD)

                for n in range(NU):
                    q_unit(0, 0, n)
                for j in range(4):
                    chunk(0, j)
                with pe.Fori(1, NHALF * LCP - 1) as at:
                    for j in range(4):
                        chunk(at, j)
                for j in range(4):
                    chunk(NHALF * LCP - 1, j, more=(j < 3))

            @block.scalar
            def _(act):
                def chunk(i4, j):
                    i = 4 * i4 + j
                    for n in range(NU):
                        act.wait_ge(q_units, NU * i + n + 1)
                        later(act, r_stored[j % 2][n * NP // NU], 16 * (2 * i4 + j // 2))
                        nc.scalar.activation(r[j % 2][:, n * QL:(n + 1) * QL, :], pq[n % 2][:], ACT.Copy).then_inc(q_out, 1)

                for j in range(4):
                    chunk(0, j)
                with act.Fori(1, NHALF * LCP) as i4:
                    for j in range(4):
                        chunk(i4, j)

            @block.vector
            def _(dve):
                def chunk(i4, j):
                    i = 4 * i4 + j
                    dve.wait_ge(q_out, NU * (i + 1))
                    for n in range(NU):
                        dve.wait_ge(k_units, NU * i + n + 1)
                        part = r[j % 2][:, :, n * KR:(n + 1) * KR]
                        nc.vector.tensor_tensor(part, pk[n % 2][:].rearrange("p r l -> p l r"), part, ALU.add
                                                ).then_inc(k_added, 1)

                for j in range(4):
                    chunk(0, j)
                with dve.Fori(1, NHALF * LCP) as i4:
                    for j in range(4):
                        chunk(i4, j)

            @block.sync
            def _(sp):
                for g in range(ng):
                    with sp.Fori(0, RH * LCP) as at:
                        i4 = at + g * RH * LCP
                        for u in range(2):
                            for v in range(2):
                                sp.wait_ge(k_added, NU * (4 * i4 + 2 * u + v + 1))
                                for p in range(NP):
                                    part = LW // NP
                                    to = r_d[g][:, bass.ds((2 * (at % LCP) + u) * LW + p * part, part),
                                                bass.ts((at // LCP) * 2 + v, RW)]
                                    sp.dma_start(to, r[v][:, p * part:(p + 1) * part, :]).then_inc(r_stored[v][p], 16)
                for v in range(2):
                    for p in range(NP):
                        sp.wait_ge(r_stored[v][p], 16 * 2 * NHALF * LCP)


def attention(nc, qf_d, ks_d, v_d, r_d, cT_d, nb=NB):
    ctx = ExitStack()
    with ctx:
        def sb(name, shape, dt=F32):
            return ctx.enter_context(nc.sbuf_tensor(name, shape, dt))

        def ps(name, shape):
            return ctx.enter_context(nc.psum_tensor(name, shape, F32))

        def sem(name):
            return ctx.enter_context(nc.semaphore(name))

        GH = 4
        CT = P // GH
        U = 2 * GH
        RR = 4
        AHEAD = 2
        BANKS = 3
        SLOTS = 2 * H
        NH, NGR = nb * H, nb * H // GH
        BG = H // GH
        ident = sb("t_ident", [P, P])
        qa = sb("t_qa", [ROWS, 1, SLOTS, S], BF16)
        kb = sb("t_kb", [ROWS, RC, SLOTS, RW], BF16)
        vv = sb("t_v", [P, 2, GH, TT, D])
        r = sb("t_r", [P, RR, TT, S])
        neg = sb("t_neg", [P, TT, S])
        low = sb("t_low", [P, 2, TT])
        e = sb("t_e", [P, 2, TT, S])
        total = sb("t_total", [P, 2, TT, GH])
        inv = sb("t_inv", [P, 2, TT, GH])
        wide = sb("t_wide", [P, TT * GH, CT])
        ones = sb("t_ones", [P, TT * GH])
        wideT = sb("t_wideT", [P, S])
        eT = sb("t_eT", [P, 2, GH, TT, TT, P])
        out = sb("t_out", [P, 2, S])
        tiny = sb("t_tiny", [P, 8])
        p_s = [ps(f"t_ps{i}", [P, S]) for i in range(BANKS)]
        p_t = [ps(f"t_pt{i}", [P, TT, P]) for i in range(BANKS)]
        p_c = ps("t_pc", [P, S])
        p_i = ps("t_pi", [P, S])

        ident_zero = sem("t_ident_zero")
        ident_done = sem("t_ident_done")
        batch_loaded = [sem(f"t_batch_loaded{i}") for i in range(2)]
        BATCH = 16 * (len(A_RUNS) + len(B_RUNS))
        v_loaded = [sem(f"t_v_loaded{i}") for i in range(2)]
        r_loaded = [sem(f"t_r_loaded{i}") for i in range(RR * TT)]
        scored = sem("t_scored")
        added = sem("t_added")
        exped = sem("t_exped")
        turned = sem("t_turned")
        even_out = sem("t_even_out")
        odd_out = sem("t_odd_out")
        pc_zero = sem("t_pc_zero")
        weighed = sem("t_weighed")
        inverted = sem("t_inverted")
        widened = sem("t_widened")
        wide_turned = sem("t_wide_turned")
        wide_out = sem("t_wide_out")
        ctx_done = sem("t_ctx_done")
        ctx_stored = [sem(f"t_ctx_stored{i}") for i in range(2)]

        def bank(j, L):
            return (TT * j + L) % BANKS

        def since(j, L):
            i = TT * j + L
            return BANKS if i >= BANKS else next(k for k in range(1, 2 * BANKS) if (i - k) % (TT * U) % BANKS == i)

        with nc.Block() as block:
            @block.gpsimd
            def _(pool):
                nc.gpsimd.memset(ones[:], 1.0).then_inc(ident_zero, 1)
                nc.gpsimd.memset(ident[:], 0.0).then_inc(ident_zero, 1)
                pool.wait_ge(ident_zero, 2)
                nc.gpsimd.affine_select(out=ident[:], in_=ident[:], compare_op=ALU.not_equal, fill=1.0,
                                        base=0, pattern=[[-1, P]], channel_multiplier=1).then_inc(ident_done, 1)

                def load(pair, u):
                    b = 2 * pair + u
                    g, b8 = b // GB, b % GB
                    for tensor, src, runs in ((qa, qf_d, A_RUNS), (kb, ks_d, B_RUNS)):
                        for row, stored, rows in runs:
                            pool.dma_start(tensor[row:row + rows, :, u * H:(u + 1) * H, :].rearrange("r n h w -> r n (h w)"),
                                           src[g, :, b8, stored:stored + rows, :, :].rearrange("n r h w -> r n (h w)")
                                           ).then_inc(batch_loaded[u], 16)

                def widen(G, par):
                    pool.wait_ge(inverted, G + 1)
                    later(pool, wide_turned, G)
                    narrow = inv[:, par].rearrange("p l j -> p (l j)").unsqueeze(2).to_broadcast([P, TT * GH, CT])
                    nc.gpsimd.tensor_tensor(wide[:], narrow, ones[:].unsqueeze(2).to_broadcast([P, TT * GH, CT]),
                                            ALU.mult).then_inc(widened, 1)

                def store(b, k):
                    pool.wait_ge(ctx_done, BG * b + k + 1)
                    for j in range(GH):
                        row = (GH * k + j) * D
                        pool.dma_start(cT_d[b, row:row + D, :], out[j * CT:j * CT + D, k % 2, :]
                                       ).then_inc(ctx_stored[k % 2], 16)

                def batch(pair, u, more=True):
                    b = 2 * pair + u
                    for k in range(BG):
                        if more or k + 1 < BG:
                            widen(BG * b + k + 1, (k + 1) % 2)
                        if more and k == BG - 1 and (not isinstance(pair, int) or b + 2 < nb):
                            pool.wait_ge(scored, TT * H * (b + 1))
                            load(pair + 1, u)
                        store(b, k)

                for u in range(2):
                    load(0, u)
                widen(0, 0)
                with pool.Fori(0, nb // 2 - 1) as pair:
                    for u in range(2):
                        batch(pair, u)
                for u in range(2):
                    batch(nb // 2 - 1, u, more=(u == 0))
                for par in range(2):
                    pool.wait_ge(ctx_stored[par], 16 * GH * NGR // 2)

            @block.sync
            def _(sp):
                def load_r(g, n, j):
                    for L in range(TT):
                        later(sp, added, TT * (n - RR) + L + 1)
                        sp.dma_start(r[:, j % RR, L, :], r_d[g][n - g * P, L * P:(L + 1) * P, :]
                                     ).then_inc(r_loaded[j % RR * TT + L], 16)

                def load_v(G, b, k):
                    later(sp, weighed, TT * (G - 1))
                    sp.dma_start(vv[:, k % 2].rearrange("p h t d -> p (h t d)"),
                                 v_d[b, :, k * GH:(k + 1) * GH].rearrange("p h t d -> p (h t d)")
                                 ).then_inc(v_loaded[k % 2], 16)

                def heads(g, b, half):
                    for j in range(U):
                        load_r(g, H * b + U * half + j, j)
                        if j % GH == GH - 1:
                            k = (U * half + j) // GH
                            load_v(BG * b + k, b, k)

                for half in range(2):
                    heads(0, 0, half)
                for g in range((nb + GB - 1) // GB):
                    with sp.Fori(max(1, g * GB), min((g + 1) * GB, nb)) as b:
                        for half in range(2):
                            heads(g, b, half)

            @block.tensor
            def _(pe):
                pe.wait_ge(ident_done, 1)
                pe.wait_ge(pc_zero, 1)

                def score(n, j, L, slot):
                    later(pe, added, TT * n + L - since(j, L) + 1)
                    nc.tensor.matmul(p_s[bank(j, L)][:], qa[:, 0, slot, L * P:(L + 1) * P], kb[:, :, slot, :],
                                     start=True, stop=True).then_inc(scored, 1)

                def turn(n, j, L):
                    t = TT * n + L
                    pe.wait_ge(exped, t + 1)
                    before = TT * j + L - since(j, L)
                    later(pe, (even_out, odd_out)[before % 2], TT // 2 * (n - j) + before // 2 + 1)
                    for c in range(TT):
                        last = nc.tensor.transpose(p_t[bank(j, L)][:, c, :], e[:, j % 2, L, c * P:(c + 1) * P], ident[:])
                    last.then_inc(turned, 1)

                def weigh(G, par, c, loads):
                    if c == 0:
                        pe.wait_ge(even_out, TT // 2 * GH * (G + 1))
                        pe.wait_ge(odd_out, TT // 2 * GH * (G + 1))
                        pe.wait_ge(v_loaded[par], 16 * loads)
                        later(pe, ctx_done, G)
                    for j in range(GH):
                        last = nc.tensor.matmul(p_c[j * CT:j * CT + D, :], vv[:, par, j, c, :],
                                                eT[:, par, j, c].rearrange("p l q -> p (l q)"),
                                                start=(c == 0), stop=(c == TT - 1))
                    last.then_inc(weighed, 1)

                def turn_wide(G, L):
                    if L == 0:
                        pe.wait_ge(widened, G + 1)
                        later(pe, wide_out, G)
                    last = nc.tensor.transpose(p_i[:, L * P:(L + 1) * P],
                                               wide[:, L * GH:(L + 1) * GH, :].rearrange("p j w -> p (j w)"), ident[:])
                    if L == TT - 1:
                        last.then_inc(wide_turned, 1)

                def head(step, j):
                    n = U * step + j
                    fixed = isinstance(n, int)
                    for L in range(TT):
                        later_head, tile = n + (L + AHEAD) // TT, (L + AHEAD) % TT
                        if not fixed or later_head < NH:
                            score(later_head, (j + (L + AHEAD) // TT) % U, tile, later_head % SLOTS)
                        if not fixed or 1 <= n <= NH:
                            turn(n - 1, (j - 1) % U, L)
                        if L == 3 and (not fixed or 5 <= n < NH + 5):
                            ahead = (j - 5) // GH
                            weigh(2 * step + ahead, ahead % 2, (j - 5) % GH, step + ahead // 2 + 1)
                        if j % GH == 2 and (not fixed or 6 <= n < NH + 6):
                            turn_wide(2 * step + (j - 6) // GH, L)

                pe.wait_ge(batch_loaded[0], BATCH)
                for L in range(AHEAD):
                    score(0, 0, L, 0)
                for step in range(H // U):
                    if step == H // U - 1:
                        pe.wait_ge(batch_loaded[1], BATCH)
                    for j in range(U):
                        head(step, j)
                with pe.Fori(H // U, NH // U - 1) as step:
                    pe.wait_ge(batch_loaded[0], BATCH * ((step + 1) // (SLOTS // U) + 1))
                    pe.wait_ge(batch_loaded[1], BATCH * ((step + 1 + H // U) // (SLOTS // U)))
                    for j in range(U):
                        head(step, j)
                for j in range(U):
                    head(NH // U - 1, j)
                for j in range(GH + 1):
                    head(NH // U, j)

            @block.vector
            def _(dve):
                nc.vector.memset(p_c[:], 0.0).then_inc(pc_zero, 1)

                def add(n, j, L, loads):
                    t = TT * n + L
                    dve.wait_ge(scored, t + 1)
                    dve.wait_ge(r_loaded[j % RR * TT + L], 16 * loads)
                    later(dve, exped, t - TT + 1)
                    nc.vector.memset(tiny[:, L:L + 1], 0.0)
                    nc.vector.tensor_tensor_reduce(out=neg[:, L, :], in0=p_s[bank(j, L)][:], in1=r[:, j % RR, L, :], scale=-0.25,
                                                   scalar=3.0e38, op0=ALU.add, op1=ALU.min,
                                                   accum_out=low[:, j % 2, L:L + 1]).then_inc(added, 1)

                def empty(n, j, L, G):
                    dve.wait_ge(turned, TT * n + L + 1)
                    later(dve, weighed, TT * (G - 1))
                    nc.vector.tensor_copy(eT[:, j // GH, j % GH, :, L, :], p_t[bank(j, L)][:]).then_inc(odd_out, 1)

                def invert(G, par):
                    dve.wait_ge(exped, TT * GH * (G + 1))
                    later(dve, widened, G - 1)
                    nc.vector.reciprocal(inv[:, par], total[:, par]).then_inc(inverted, 1)

                def scale(G, par, stores):
                    dve.wait_ge(weighed, TT * (G + 1))
                    dve.wait_ge(wide_out, G + 1)
                    later(dve, ctx_stored[par], 16 * GH * stores)
                    nc.vector.tensor_tensor(out[:, par, :], p_c[:], wideT[:], ALU.mult).then_inc(ctx_done, 1)

                def head(step, j):
                    n = U * step + j
                    fixed = isinstance(n, int)
                    for L in range(TT):
                        if not fixed or n < NH:
                            add(n, j, L, 2 * step + j // RR + 1)
                        if L == 1 and (not fixed or 2 <= n <= NH + 1):
                            empty(n - 2, (j - 2) % U, 3, 2 * step + (j - 2) // GH)
                        if L == 3 and (not fixed or 1 <= n <= NH):
                            empty(n - 1, (j - 1) % U, 1, 2 * step + (j - 1) // GH)
                        if j % GH == 0 and L == 1 and (not fixed or 4 <= n <= NH):
                            invert(2 * step + j // GH - 1, (j // GH - 1) % 2)
                        if j % GH == 1 and L == 1 and (not fixed or 9 <= n):
                            scale(2 * step + j // GH - 2, j // GH, step - 1)

                for step in range(2):
                    for j in range(U):
                        head(step, j)
                with dve.Fori(2, NH // U) as step:
                    for j in range(U):
                        head(step, j)
                for j in range(GH + 2):
                    head(NH // U, j)

            @block.scalar
            def _(act):
                def exp(n, j, L, G):
                    t = TT * n + L
                    act.wait_ge(added, t + 1)
                    later(act, turned, t - 2 * TT + 1)
                    if L == 0 and j % GH == 0:
                        later(act, inverted, G - 1)
                    nc.scalar.activation(e[:, j % 2, L, :], neg[:, L, :], ACT.Exp, bias=low[:, j % 2, L:L + 1], scale=-1.0,
                                         accum_out=total[:, j // GH, L, j % GH:j % GH + 1]).then_inc(exped, 1)

                def empty(n, j, L, G):
                    act.wait_ge(turned, TT * n + L + 1)
                    later(act, weighed, TT * (G - 1))
                    nc.scalar.activation(eT[:, j // GH, j % GH, :, L, :], p_t[bank(j, L)][:], ACT.Copy).then_inc(even_out, 1)

                def empty_wide(G):
                    act.wait_ge(wide_turned, G + 1)
                    later(act, ctx_done, G)
                    nc.scalar.activation(wideT[:], p_i[:], ACT.Copy).then_inc(wide_out, 1)

                def head(step, j):
                    n = U * step + j
                    fixed = isinstance(n, int)
                    for L in range(TT):
                        if L == 0 and (not fixed or 2 <= n <= NH + 1):
                            empty(n - 2, (j - 2) % U, 2, 2 * step + (j - 2) // GH)
                        if L == 2 and (not fixed or 1 <= n <= NH):
                            empty(n - 1, (j - 1) % U, 0, 2 * step + (j - 1) // GH)
                        if not fixed or n < NH:
                            exp(n, j, L, 2 * step + j // GH)
                        if j % GH == 3 and L == 1 and (not fixed or 7 <= n):
                            empty_wide(2 * step + j // GH - 1)

                for step in range(2):
                    for j in range(U):
                        head(step, j)
                with act.Fori(2, NH // U) as step:
                    for j in range(U):
                        head(step, j)
                for j in range(GH):
                    head(NH // U, j)


def experts(nc, ins, mod_d, h_d, cT_d, out, nb=NB):
    ctx = ExitStack()
    with ctx:
        def sb(name, shape, dt=F32):
            return ctx.enter_context(nc.sbuf_tensor(name, shape, dt))

        def ps(name, shape):
            return ctx.enter_context(nc.psum_tensor(name, shape, F32))

        def sem(name):
            return ctx.enter_context(nc.semaphore(name))

        EP = NE // 2
        ident = sb("e_ident", [P, P])
        wo = sb("e_wo", [P, KC, E])
        bo = sb("e_bo", [P, E])
        wr = sb("e_wr", [P, KC, NE])
        br = sb("e_br", [P, NE])
        we = sb("e_we", [P, KC, NE * E])
        be = sb("e_be", [NE, E])
        number = sb("e_number", [P, NE])
        h = sb("e_h", [P, 2, TT, E])
        x = sb("e_x", [P, 2, TT, E])
        md = sb("e_mod", [P, 2, 4, E])
        gb = sb("e_gb", [P, 2, E])
        cT = sb("e_cT", [P, 2, KC, S])
        hb = sb("e_hb", [P, 2, TT, E])
        xb = sb("e_xb", [P, 2, TT, E])
        a = sb("e_a", [P, TT, E])
        st = sb("e_stats", [P, TT, 6])
        mv = sb("e_mv", [P, TT, 2])
        var = sb("e_var", [P, TT])
        root = sb("e_root", [P, TT])
        inv = sb("e_inv", [P, TT])
        tmp = sb("e_tmp", [P, TT])
        an = sb("e_an", [P, TT, E])
        x1 = sb("e_x1", [P, 2, TT, E])
        h2 = sb("e_h2", [P, TT, E])
        h2T = sb("e_h2T", [P, 2, KC, S])
        lg = sb("e_logits", [P, TT, NE])
        best = sb("e_best", [P, TT, NE])
        at = sb("e_at", [P, TT, NE], U32)
        atf = sb("e_atf", [P, TT, NE])
        first = sb("e_first", [P, TT, NE])
        second = sb("e_second", [P, TT, NE])
        mask = sb("e_mask", [P, 2, TT, NE])
        mT = sb("e_maskT", [NE, TT, P])
        even = sb("e_even", [P, 2, TT, E])
        odd = sb("e_odd", [P, 2, TT, E])
        last_two = sb("e_last_two", [P, 2, TT, 2, E])
        y = sb("e_y", [P, 2, TT, E])
        pT = ps("e_pT", [P, KC, S])
        pA = ps("e_pA", [P, TT, E])
        pX = [ps(f"e_pX{i}", [P, 2, E]) for i in range(EP)]
        pR = pT[:, 0, 0:TT * NE].rearrange("p (t e) -> p t e", t=TT)
        pM = pT[0:NE, 1, :].rearrange("e (t p) -> e t p", t=TT)

        ident_zero = sem("e_ident_zero")
        ident_done = sem("e_ident_done")
        wo_loaded = sem("e_wo_loaded")
        bo_loaded = sem("e_bo_loaded")
        w_loaded = sem("e_w_loaded")
        NW = 16 * 5
        ctx_loaded = [sem(f"e_ctx_loaded{u}") for u in range(2)]
        in_loaded = [sem(f"e_in_loaded{u}") for u in range(2)]
        gb_loaded = [sem(f"e_gb_loaded{u}") for u in range(2)]
        attn_done = sem("e_attn_done")
        sums_done = sem("e_sums_done")
        a_done = sem("e_a_done")
        step = sem("e_step")
        root_in = sem("e_root_in")
        root_out = sem("e_root_out")
        x1_done = sem("e_x1_done")
        h2_done = sem("e_h2_done")
        h2_turned = sem("e_h2_turned")
        h2T_out = sem("e_h2T_out")
        routed = sem("e_routed")
        r_step = sem("e_r_step")
        mask_done = sem("e_mask_done")
        mask_turned = sem("e_mask_turned")
        mT_out = sem("e_mT_out")
        bias_done = sem("e_bias_done")
        bias_out = sem("e_bias_out")
        x_unit = sem("e_x_unit")
        even_step = sem("e_even_step")
        odd_step = sem("e_odd_step")
        last_two_done = sem("e_last_two_done")
        NV = EP - 1
        NY = 4
        y_step = sem("e_y_step")
        y_done = sem("e_y_done")
        y_stored = [sem(f"e_y_stored{u}") for u in range(2)]

        x_v = ins["x"].rearrange("b (t p) e -> b p t e", p=P)
        h_v = h_d.rearrange("b (t p) e -> b p t e", p=P)
        out_v = out.rearrange("b (t p) e -> b p t e", p=P)

        def batches(engine, before, each, after):
            before()
            for u in range(2):
                each(0, u)
            with engine.Fori(1, nb // 2 - 1) as pair:
                for u in range(2):
                    each(pair, u)
            each(nb // 2 - 1, 0)
            after()

        with nc.Block() as block:
            @block.sync
            def _(sp):
                def load(pair, u):
                    b = 2 * pair + u
                    later(sp, attn_done, b - 1)
                    sp.dma_start(cT[:, u], cT_d[b].rearrange("(k p) l -> p k l", p=P)).then_inc(ctx_loaded[u], 16)
                    later(sp, sums_done, 2 * (b - 1))
                    sp.dma_start(h[:, u], h_v[b]).then_inc(in_loaded[u], 16)
                    sp.dma_start(x[:, u], x_v[b]).then_inc(in_loaded[u], 16)
                    later(sp, h2_done, b - 1)
                    sp.dma_start(md[:, u], mod_d[b, GAG:CB1 + 1, :].partition_broadcast(P)).then_inc(in_loaded[u], 16)

                def load_gate(pair, u):
                    b = 2 * pair + u
                    later(sp, y_done, b - 1)
                    sp.dma_start(gb[:, u], mod_d[b, GB_, :].partition_broadcast(P)).then_inc(gb_loaded[u], 16)

                sp.dma_start(wo[:], ins["wo"].rearrange("(k p) n -> p k n", p=P)).then_inc(wo_loaded, 16)
                sp.dma_start(bo[:], ins["bo"].partition_broadcast(P)).then_inc(bo_loaded, 16)
                load(0, 0)
                sp.dma_start(wr[:], ins["wr"].rearrange("(k p) n -> p k n", p=P)).then_inc(w_loaded, 16)
                sp.dma_start(br[:], ins["br"].partition_broadcast(P)).then_inc(w_loaded, 16)
                sp.dma_start(be[:], ins["be"]).then_inc(w_loaded, 16)
                for k in range(KC):
                    sp.dma_start(we[:, k, :], ins["we"][k * P:(k + 1) * P, :]).then_inc(w_loaded, 16)
                load(0, 1)
                load_gate(0, 0)
                load_gate(0, 1)
                with sp.Fori(1, nb // 2) as pair:
                    for u in range(2):
                        load(pair, u)
                        load_gate(pair, u)

            @block.gpsimd
            def _(pool):
                nc.gpsimd.memset(ident[:], 0.0).then_inc(ident_zero, 1)
                pool.wait_ge(ident_zero, 1)
                nc.gpsimd.affine_select(out=ident[:], in_=ident[:], compare_op=ALU.not_equal, fill=1.0,
                                        base=0, pattern=[[-1, P]], channel_multiplier=1).then_inc(ident_done, 1)
                pool.wait_ge(bo_loaded, 16)

                def sums(pair, u):
                    b = 2 * pair + u
                    pool.wait_ge(in_loaded[u], 48 * (pair + 1))
                    later(pool, a_done, b - 1)
                    later(pool, x1_done, b - 1)
                    nc.gpsimd.tensor_tensor(hb[:, u], h[:, u], bo[:].unsqueeze(1).to_broadcast([P, TT, E]), ALU.add
                                            ).then_inc(sums_done, 1)
                    nc.gpsimd.tensor_tensor(xb[:, u], x[:, u], md[:, u, 1:2, :].to_broadcast([P, TT, E]), ALU.add).then_inc(sums_done, 1)

                def finish(pair, u):
                    b = 2 * pair + u
                    pool.wait_ge(even_step, TT * NV * (b + 1))
                    pool.wait_ge(odd_step, TT * NV * (b + 1))
                    pool.wait_ge(last_two_done, TT * (b + 1))
                    pool.wait_ge(gb_loaded[u], 16 * (pair + 1))
                    later(pool, y_stored[u], 16 * pair)
                    nc.gpsimd.tensor_tensor(y[:, u], even[:, u], odd[:, u], ALU.add).then_inc(y_step, 1)
                    for i in range(2):
                        pool.wait_ge(y_step, NY * b + i + 1)
                        nc.gpsimd.tensor_tensor(y[:, u], y[:, u], last_two[:, u, :, i, :], ALU.add).then_inc(y_step, 1)
                    pool.wait_ge(y_step, NY * b + 3)
                    nc.gpsimd.tensor_tensor(y[:, u], y[:, u], gb[:, u:u + 1, :].to_broadcast([P, TT, E]), ALU.mult
                                            ).then_inc(y_step, 1)
                    pool.wait_ge(y_step, NY * (b + 1))
                    nc.gpsimd.tensor_tensor(y[:, u], y[:, u], x1[:, u], ALU.add).then_inc(y_done, 1)
                    pool.wait_ge(y_done, b + 1)
                    pool.dma_start(out_v[b], y[:, u]).then_inc(y_stored[u], 16)

                def before():
                    sums(0, 0)
                    sums(0, 1)

                def each(pair, u):
                    if not isinstance(pair, int) or 2 * pair + u + 2 < nb:
                        sums(pair + 1, u)
                    finish(pair, u)

                batches(pool, before, each, lambda: finish(nb // 2 - 1, 1))
                for u in range(2):
                    pool.wait_ge(y_stored[u], 16 * (nb // 2))

            @block.tensor
            def _(pe):
                pe.wait_ge(ident_done, 1)
                pe.wait_ge(wo_loaded, 16)

                def project(pair, u):
                    b = 2 * pair + u
                    pe.wait_ge(ctx_loaded[u], 16 * (pair + 1))
                    later(pe, bias_out, b)
                    for t in range(TT):
                        for k in range(KC):
                            last = nc.tensor.matmul(pA[:, t, :], cT[:, u, k, t * P:(t + 1) * P], wo[:, k, :],
                                                    start=(k == 0), stop=(k == KC - 1))
                    last.then_inc(attn_done, 1)

                def turn_h2(pair, u):
                    pe.wait_ge(h2_done, 2 * pair + u + 1)
                    later(pe, mT_out, 2 * pair + u)
                    for t in range(TT):
                        for c in range(KC):
                            last = nc.tensor.transpose(pT[:, c, t * P:(t + 1) * P], h2[:, t, c * P:(c + 1) * P], ident[:])
                    last.then_inc(h2_turned, 1)

                def route(pair, u):
                    pe.wait_ge(h2T_out, 2 * pair + u + 1)
                    for t in range(TT):
                        for k in range(KC):
                            last = nc.tensor.matmul(pR[:, t, :], h2T[:, u, k, t * P:(t + 1) * P], wr[:, k, :],
                                                    start=(k == 0), stop=(k == KC - 1))
                    last.then_inc(routed, 1)

                def turn_mask(pair, u):
                    pe.wait_ge(mask_done, 2 * pair + u + 1)
                    for t in range(TT):
                        last = nc.tensor.transpose(pM[:, t, :], mask[:, u, t, :], ident[:])
                    last.then_inc(mask_turned, 1)

                def biases(pair, u):
                    b = 2 * pair + u
                    pe.wait_ge(mT_out, b + 1)
                    pe.wait_ge(a_done, b + 1)
                    for t in range(TT):
                        last = nc.tensor.matmul(pA[:, t, :], mT[:, t, :], be[:], start=True, stop=True)
                    last.then_inc(bias_done, 1)

                def expert(pair, u, t, first, last_n):
                    b = 2 * pair + u
                    for n in range(first, last_n):
                        before = TT * b + t - 1
                        if n < NV:
                            later(pe, even_step, NV * before + n + 1)
                            later(pe, odd_step, NV * before + n + 1)
                        else:
                            later(pe, last_two_done, before + 1)
                        for k in range(KC):
                            last = nc.tensor.matmul(pX[n][:], h2T[:, u, k, t * P:(t + 1) * P],
                                                    we[:, k, n * 2 * E:(n + 1) * 2 * E], start=(k == 0), stop=(k == KC - 1))
                        last.then_inc(x_unit, 1)

                def before():
                    project(0, 0)
                    pe.wait_ge(w_loaded, NW)
                    turn_h2(0, 0)
                    route(0, 0)

                def body(pair, u, more=True):
                    nxt = (pair, 1) if u == 0 else (pair + 1, 0)
                    turn_mask(pair, u)
                    expert(pair, u, 0, 0, 1)
                    biases(pair, u)
                    expert(pair, u, 0, 1, 2)
                    if more:
                        project(*nxt)
                    expert(pair, u, 0, 2, EP)
                    expert(pair, u, 1, 0, EP)
                    expert(pair, u, 2, 0, EP)
                    if more:
                        turn_h2(*nxt)
                    expert(pair, u, 3, 0, 1)
                    if more:
                        route(*nxt)
                    expert(pair, u, 3, 1, EP)

                def each(pair, u):
                    body(pair, u)

                def after():
                    body(nb // 2 - 1, 1, more=False)

                batches(pe, before, each, after)

            @block.scalar
            def _(act):
                def take_root(pair, u, i):
                    act.wait_ge(root_in, 2 * (2 * pair + u) + i + 1)
                    nc.scalar.activation(root[:], var[:], ACT.Sqrt).then_inc(root_out, 1)

                def empty(pair, u):
                    b = 2 * pair + u
                    act.wait_ge(h2_turned, b + 1)
                    later(act, x_unit, TT * EP * (b - 1))
                    nc.scalar.activation(h2T[:, u], pT[:], ACT.Copy).then_inc(h2T_out, 1)

                def take_last_two(pair, u, t):
                    b = 2 * pair + u
                    if t == 0:
                        later(act, y_done, b - 1)
                    act.wait_ge(x_unit, EP * (TT * b + t + 1))
                    for i in range(2):
                        last = nc.scalar.activation(last_two[:, u, t, i, :], pX[EP - 1][:, i, :], ACT.Copy,
                                                    scale=mask[:, u, t, NE - 2 + i:NE - 1 + i])
                    last.then_inc(last_two_done, 1)

                def body(pair, u, more=True):
                    b = 2 * pair + u
                    nxt = (pair, 1) if u == 0 else (pair + 1, 0)
                    act.wait_ge(mask_turned, b + 1)
                    later(act, bias_done, b)
                    nc.scalar.activation(mT[:], pM, ACT.Copy).then_inc(mT_out, 1)
                    act.wait_ge(bias_done, b + 1)
                    later(act, y_step, NY * (b - 2) + 1)
                    nc.scalar.activation(even[:, u], pA[:], ACT.Copy).then_inc(bias_out, 1)
                    if more:
                        take_root(*nxt, 0)
                    take_last_two(pair, u, 0)
                    take_last_two(pair, u, 1)
                    if more:
                        take_root(*nxt, 1)
                    take_last_two(pair, u, 2)
                    if more:
                        empty(*nxt)
                    take_last_two(pair, u, 3)

                def before():
                    take_root(0, 0, 0)
                    take_root(0, 0, 1)
                    empty(0, 0)

                batches(act, before, body, lambda: body(nb // 2 - 1, 1, more=False))

            @block.vector
            def _(dve):
                NSTEP = 8
                for e in range(NE):
                    last = nc.vector.memset(number[:, e:e + 1], float(e))
                last.then_inc(r_step, 1)

                def normalise(src, factor, term, dst, eps, b, i, free, between=lambda: None):
                    count = [0]

                    def then(instruction):
                        count[0] += 1
                        instruction.then_inc(step, 1)
                        dve.wait_ge(step, NSTEP * (2 * b + i) + count[0])

                    def root_of():
                        dve.wait_ge(root_out, 2 * b + i + 1)

                    for t in range(TT):
                        last = nc.vector.bn_stats(st[:, t, :], src[:, t, :])
                    then(last)
                    nc.vector.memset(tmp[:], 0.0)
                    for t in range(TT):
                        last = nc.vector.bn_aggr(mv[:, t, :], st[:, t, :])
                    then(last)
                    nc.vector.tensor_scalar_add(var[:], mv[:, :, 1], eps).then_inc(root_in, 1)
                    inverse_root(nc, then, inv[:], var[:], root_of, root[:], tmp[:])
                    between()
                    for t in range(TT):
                        last = nc.vector.scalar_tensor_tensor(an[:, t, :], src[:, t, :], mv[:, t, 0:1], factor,
                                                              ALU.subtract, ALU.mult)
                    then(last)
                    free()
                    for t in range(TT):
                        last = nc.vector.scalar_tensor_tensor(dst[:, t, :], an[:, t, :], inv[:, t:t + 1], term(t),
                                                              ALU.mult, ALU.add)
                    assert count[0] == NSTEP
                    return last

                def attn_norm(pair, u, between=lambda: None):
                    b = 2 * pair + u
                    dve.wait_ge(attn_done, b + 1)
                    dve.wait_ge(sums_done, 2 * (b + 1))
                    later(dve, h2_done, b)
                    nc.vector.tensor_tensor(a[:], pA[:], hb[:, u], ALU.add).then_inc(a_done, 1)
                    dve.wait_ge(a_done, b + 1)
                    normalise(a, md[:, u, 0, :], lambda t: xb[:, u, t, :], x1[:, u], EPS_ATTN, b, 0,
                              lambda: later(dve, y_done, b - 1), between).then_inc(x1_done, 1)

                def x1_norm(pair, u):
                    b = 2 * pair + u
                    dve.wait_ge(x1_done, b + 1)
                    normalise(x1[:, u], md[:, u, 3, :], lambda t: md[:, u, 2, :], h2, EPS_LN, b, 1,
                              lambda: later(dve, h2_turned, b)).then_inc(h2_done, 1)

                def route(pair, u):
                    b = 2 * pair + u
                    count = [0]

                    def then(instruction):
                        count[0] += 1
                        instruction.then_inc(r_step, 1)
                        dve.wait_ge(r_step, 1 + 7 * b + count[0])

                    dve.wait_ge(routed, b + 1)
                    then(nc.vector.tensor_tensor(lg[:], pR, br[:].unsqueeze(1).to_broadcast([P, TT, NE]), ALU.add))
                    nc.vector.memset(tmp[:], 0.0)
                    for t in range(TT):
                        last = nc.vector.max(best[:, t, :], lg[:, t, :])
                    then(last)
                    nc.vector.memset(tmp[:], 0.0)
                    for t in range(TT):
                        last = nc.vector.max_index(at[:, t, :], best[:, t, :], lg[:, t, :])
                    then(last)
                    then(nc.vector.tensor_copy(atf[:], at[:]))
                    num = number[:].unsqueeze(1).to_broadcast([P, TT, NE])
                    then(nc.vector.tensor_tensor(first[:], num, atf[:, :, 0:1].to_broadcast([P, TT, NE]), ALU.is_equal))
                    then(nc.vector.tensor_tensor(second[:], num, atf[:, :, 1:2].to_broadcast([P, TT, NE]), ALU.is_equal))
                    then(nc.vector.tensor_tensor(mask[:, u], first[:], second[:], ALU.add))
                    dve.sem_inc(mask_done, 1)

                def combine(pair, u, t, first=0, last_n=NV):
                    b = 2 * pair + u
                    if t == 0 and first == 0:
                        dve.wait_ge(bias_out, b + 1)
                        later(dve, y_step, NY * (b - 2) + 1)
                    for n in range(first, last_n):
                        tile = TT * b + t
                        dve.wait_ge(x_unit, EP * tile + n + 1)
                        m = mask[:, u, t, :]
                        if n:
                            dve.wait_ge(even_step, NV * tile + n)
                        nc.vector.scalar_tensor_tensor(even[:, u, t, :], pX[n][:, 0, :], m[:, 2 * n:2 * n + 1],
                                                       even[:, u, t, :], ALU.mult, ALU.add).then_inc(even_step, 1)
                        if n:
                            dve.wait_ge(odd_step, NV * tile + n)
                            nc.vector.scalar_tensor_tensor(odd[:, u, t, :], pX[n][:, 1, :], m[:, 2 * n + 1:2 * n + 2],
                                                           odd[:, u, t, :], ALU.mult, ALU.add).then_inc(odd_step, 1)
                        else:
                            nc.vector.tensor_scalar(odd[:, u, t, :], pX[n][:, 1, :], m[:, 1:2], None, ALU.mult
                                                    ).then_inc(odd_step, 1)

                def before():
                    attn_norm(0, 0)
                    x1_norm(0, 0)
                    dve.wait_ge(w_loaded, NW)
                    route(0, 0)

                def each(pair, u):
                    nxt = (pair, 1) if u == 0 else (pair + 1, 0)
                    combine(pair, u, 0, 0, 2)
                    attn_norm(*nxt, lambda: combine(pair, u, 0, 2, NV))
                    combine(pair, u, 1)
                    x1_norm(*nxt)
                    combine(pair, u, 2)
                    combine(pair, u, 3, 0, 1)
                    route(*nxt)
                    combine(pair, u, 3, 1, NV)

                def after():
                    for t in range(TT):
                        combine(nb // 2 - 1, 1, t)

                batches(dve, before, each, after)


def program(nc, ins, out):
    def scratch(name, shape, dt=F32):
        return nc.dram_tensor(name, shape, dt, kind="Internal").ap()

    mod_d = scratch("mod_scratch", [NB, NMOD, E])
    tab_d = scratch("table_scratch", [ROWS, TAB], BF16)
    h_d = scratch("h_scratch", [NB, S, E])
    v_d = scratch("v_scratch", [NB, P, H, TT, D])
    qs_d = scratch("q_chunks_scratch", [NG, LC, GB, SD, H, LW], BF16)
    ks_d = scratch("k_chunks_scratch", [NG, RC, GB, SD, H, RW], BF16)
    qf_d = scratch("q_rows_scratch", [NG, 1, GB, SD, H, S], BF16)
    cT_d = scratch("ctx_scratch", [NB, E, S])
    r_d = [scratch(f"r{g}_scratch", [P * RPITCH]).rearrange("(n q) -> n q", q=RPITCH)[:, 0:S * S]
           .rearrange("n (l r) -> n l r", r=S) for g in range(NG)]
    modulation(nc, ins, mod_d, tab_d)
    projections(nc, ins, mod_d, h_d, qs_d, ks_d, qf_d, v_d)
    distances(nc, tab_d, qs_d, ks_d, r_d)
    attention(nc, qf_d, ks_d, v_d, r_d, cT_d)
    experts(nc, ins, mod_d, h_d, cT_d, out)


def kernel(**inputs):
    import numpy as np
    import concourse.bacc as bacc
    from concourse.bass_utils import run_bass_kernel_spmd

    a = {n: np.asarray(v) for n, v in inputs.items()}

    def attn(name):
        return a["L0_attn_" + name]

    def by_d(w):
        return w.reshape(-1, H, D).transpose(0, 2, 1).reshape(-1, E)

    arrays = {
        "x": attn("hidden_states"), "cT": a["L0_c"].T, "wmod": a["L0_wmod"], "eT": attn("dist_emb").T,
        "gamma": attn("ln_gamma"), "beta": attn("ln_beta"),
        "wq": by_d(attn("Wq")), "wk": by_d(attn("Wk")),
        "bq": by_d(attn("bq")).reshape(KC, P).T, "bk": by_d(attn("bk")).reshape(KC, P).T,
        "wv": attn("Wv"), "bv": attn("bv"), "wo": attn("Wo"), "bo": attn("bo"),
        "wr": a["L0_ffn_w_router"].T, "br": a["L0_ffn_b_router"],
        "we": a["L0_ffn_w_experts"].transpose(2, 0, 1).reshape(E, NE * E), "be": a["L0_ffn_b_experts"],
    }
    nc = bacc.Bacc("TRN2", target_bir_lowering=False, num_devices=1)
    maps, ins = {}, {}
    for name, array in arrays.items():
        array = np.ascontiguousarray(array)
        maps["in_" + name] = array
        ins[name] = nc.dram_tensor("in_" + name, array.shape, mybir.dt.from_np(array.dtype), kind="ExternalInput").ap()
    out = nc.dram_tensor("out_x", (NB, S, E), F32, kind="ExternalOutput").ap()
    program(nc, ins, out)
    return run_bass_kernel_spmd(nc, [maps], core_ids=[0]).results[0]["out_x"]
```
